# Optimizing a Trainium2 kernel written in Bass

```python
import numpy as np
import jax
import jax.numpy as jnp

def _softmax(x, axis=-1):
    return jax.nn.softmax(x, axis=axis)

def _gelu(x):
    return jax.nn.gelu(x, approximate=True)

def _silu(x):
    return jax.nn.silu(x)

def _sigmoid(x):
    return jax.nn.sigmoid(x)

def _layernorm(x, axis=-1, eps=1e-05):
    m = jnp.mean(x, axis=axis, keepdims=True)
    v = jnp.var(x, axis=axis, keepdims=True)
    return (x - m) / jnp.sqrt(v + eps)

def _scatter_add(tgt, idx, src, axis=0):
    return tgt.at[idx].add(src)

def _segment_sum(src, seg, n):
    return jax.ops.segment_sum(src, seg, n)
kernel_name = 'mk_flamingo_gated_d1_seqx_r4_eebb69'

def setup_inputs(seed: int=0):
    np.random.seed(seed)
    _w = jnp.asarray

    def _rec_inputs():
        import jax
        import jax.numpy as jnp
        _rk = jax.random.key(seed)
        x = -0.0003929 + 0.9999 * jax.random.normal(jax.random.fold_in(_rk, 1), (8, 256, 256), jnp.float32)
        _lenS = 256 - jax.random.randint(jax.random.fold_in(_rk, 7), (8,), 0, max(1, 256 // 4) + 1, jnp.int32)
        _lenS2 = 256 - jax.random.randint(jax.random.fold_in(_rk, 8), (8,), 0, max(1, 256 // 4) + 1, jnp.int32)
        _ctx_1024P = jax.random.normal(jax.random.fold_in(_rk, 11), (8, 16, 256), jnp.float32)
        _ctx_1024c = jax.random.dirichlet(jax.random.fold_in(_rk, 511), 0.3 * jnp.ones((16,), jnp.float32), (8, 256))
        _ctx_1024t = jnp.einsum('bsk,bkd->bsd', _ctx_1024c, _ctx_1024P)
        _ctx_1024t = _ctx_1024t * jax.lax.rsqrt(jnp.mean(jnp.square(_ctx_1024t)) + 1e-12) * 0.953939
        ctx_1024 = 2.81802e-05 + 1.00001 * (_ctx_1024t + 0.3 * jax.random.normal(jax.random.fold_in(_rk, 611), (8, 256, 256), jnp.float32))
        _g = jax.random.normal(jax.random.fold_in(_rk, 9001), (2, 1), jnp.float32)
        _g = jnp.sign(_g) * jnp.maximum(jnp.abs(_g), 1.0) + (_g == 0) * 1.0
        g_xattn = _g[0]
        g_ffn = _g[1]
        return (x, ctx_1024, g_xattn, g_ffn)
    x, ctx_1024, g_xattn, g_ffn = _rec_inputs()

    def _L0_xattn_setup():
        import jax, jax.numpy as jnp
        import numpy as np
        B_SZ, T_LEN, C_DIM = (4, 1024, 256)

        def _wkv_scan(ek, v, ew):

            def step(carry, xt):
                A, Bd = carry
                ekt, vt = xt
                out = (A, Bd)
                A2 = ew * A + ekt * vt
                B2 = ew * Bd + ekt
                return ((A2, B2), out)
            init = (jnp.zeros_like(ek[:, 0]), jnp.zeros_like(ek[:, 0]))
            xs = (jnp.moveaxis(ek, 1, 0), jnp.moveaxis(v, 1, 0))
            _, (A, Bd) = jax.lax.scan(step, init, xs)
            return (jnp.moveaxis(A, 0, 1), jnp.moveaxis(Bd, 0, 1))

        def _birwkv(r, k, v, w, u):
            wc = w.reshape(-1)
            uc = u.reshape(-1)
            ew = jnp.exp(wc)
            ek = jnp.exp(k)
            Af, Bf = _wkv_scan(ek, v, ew)
            Ab, Bb = _wkv_scan(ek[:, ::-1], v[:, ::-1], ew)
            Ab = Ab[:, ::-1]
            Bb = Bb[:, ::-1]
            cur = jnp.exp(uc + k)
            wkv = (Af + Ab + cur * v) / (Bf + Bb + cur)
            return jax.nn.sigmoid(r) * wkv
        key = jax.random.key(seed)
        k1, k2, k3, k4, k5 = jax.random.split(key, 5)
        r = jax.random.normal(k1, (B_SZ, T_LEN, C_DIM), dtype=jnp.float32)
        k = jax.random.normal(k2, (B_SZ, T_LEN, C_DIM), dtype=jnp.float32)
        v = jax.random.normal(k3, (B_SZ, T_LEN, C_DIM), dtype=jnp.float32)
        w = -(0.3 + jax.random.uniform(k4, (1, 1, C_DIM), dtype=jnp.float32))
        u = jax.random.normal(k5, (1, 1, C_DIM), dtype=jnp.float32) * 0.1
        return {'r': r, 'k': k, 'v': v, 'w': w, 'u': u}
    _L0_xattn_all = _L0_xattn_setup()
    _L0_xattn_in = {k: v for k, v in _L0_xattn_all.items() if k in ('w', 'u')}
    del _L0_xattn_all

    def _L0_ffn_setup():
        import jax, jax.numpy as jnp
        import numpy as np
        import math
        E = 16
        TOP_K = 2
        D = 256
        F = 1024
        SH = 512
        key = jax.random.key(seed)
        ks = jax.random.split(key, 10)
        s = lambda k, shape, fan: jax.random.normal(k, shape, jnp.float32) / np.sqrt(fan)
        return {'x': jax.random.normal(ks[0], (32, 64, D), jnp.float32), 'gate_w': s(ks[1], (E, D), D), 'up_w': s(ks[2], (E, F, D), D), 'up_b': s(ks[3], (E, F), D), 'gw': s(ks[4], (E, F, D), D), 'gb': s(ks[5], (E, F), D), 'down_w': s(ks[6], (E, D, F), F), 'down_b': s(ks[7], (E, D), F), 'sh_gate_w': s(ks[8], (SH, D), D), 'sh_up_w': s(ks[9], (SH, D), D), 'sh_down_w': s(jax.random.fold_in(key, 11), (D, SH), SH)}
    _L0_ffn_all = _L0_ffn_setup()
    _L0_ffn_in = {k: v for k, v in _L0_ffn_all.items() if k in ('gate_w', 'up_w', 'up_b', 'gw', 'gb', 'down_w', 'down_b', 'sh_gate_w', 'sh_up_w', 'sh_down_w')}
    del _L0_ffn_all
    return {'x': x, 'ctx_1024': ctx_1024, 'g_xattn': g_xattn, 'g_ffn': g_ffn, 'L0_xattn_w': _L0_xattn_in['w'], 'L0_xattn_u': _L0_xattn_in['u'], 'L0_ffn_gate_w': _L0_ffn_in['gate_w'], 'L0_ffn_up_w': _L0_ffn_in['up_w'], 'L0_ffn_up_b': _L0_ffn_in['up_b'], 'L0_ffn_gw': _L0_ffn_in['gw'], 'L0_ffn_gb': _L0_ffn_in['gb'], 'L0_ffn_down_w': _L0_ffn_in['down_w'], 'L0_ffn_down_b': _L0_ffn_in['down_b'], 'L0_ffn_sh_gate_w': _L0_ffn_in['sh_gate_w'], 'L0_ffn_sh_up_w': _L0_ffn_in['sh_up_w'], 'L0_ffn_sh_down_w': _L0_ffn_in['sh_down_w']}

def reference(x, ctx_1024, g_xattn, g_ffn, L0_xattn_w, L0_xattn_u, L0_ffn_gate_w, L0_ffn_up_w, L0_ffn_up_b, L0_ffn_gw, L0_ffn_gb, L0_ffn_down_w, L0_ffn_down_b, L0_ffn_sh_gate_w, L0_ffn_sh_up_w, L0_ffn_sh_down_w):
    import jax
    import jax.numpy as jnp

    def _L0_xattn_ref(r, k, v, w, u):
        import jax, jax.numpy as jnp
        import numpy as np
        B_SZ, T_LEN, C_DIM = (4, 1024, 256)

        def _wkv_scan(ek, v, ew):

            def step(carry, xt):
                A, Bd = carry
                ekt, vt = xt
                out = (A, Bd)
                A2 = ew * A + ekt * vt
                B2 = ew * Bd + ekt
                return ((A2, B2), out)
            init = (jnp.zeros_like(ek[:, 0]), jnp.zeros_like(ek[:, 0]))
            xs = (jnp.moveaxis(ek, 1, 0), jnp.moveaxis(v, 1, 0))
            _, (A, Bd) = jax.lax.scan(step, init, xs)
            return (jnp.moveaxis(A, 0, 1), jnp.moveaxis(Bd, 0, 1))

        def _birwkv(r, k, v, w, u):
            wc = w.reshape(-1)
            uc = u.reshape(-1)
            ew = jnp.exp(wc)
            ek = jnp.exp(k)
            Af, Bf = _wkv_scan(ek, v, ew)
            Ab, Bb = _wkv_scan(ek[:, ::-1], v[:, ::-1], ew)
            Ab = Ab[:, ::-1]
            Bb = Bb[:, ::-1]
            cur = jnp.exp(uc + k)
            wkv = (Af + Ab + cur * v) / (Bf + Bb + cur)
            return jax.nn.sigmoid(r) * wkv
        return _birwkv(r, k, v, w, u)

    def _L0_ffn_ref(x, gate_w, up_w, up_b, gw, gb, down_w, down_b, sh_gate_w, sh_up_w, sh_down_w):
        import jax, jax.numpy as jnp
        import numpy as np
        import math
        E = 16
        TOP_K = 2
        D = 256
        F = 1024
        SH = 512
        B, S, Dm = x.shape
        h = x.reshape(-1, Dm)
        T = h.shape[0]
        scores = jax.nn.sigmoid(h @ gate_w.T)
        cap = math.ceil(T / E * TOP_K)
        topk_score, topk_ids = jax.lax.top_k(scores.T, cap)
        xin = h[topk_ids]
        up = jnp.einsum('ecd,efd->ecf', xin, up_w) + up_b[:, None, :]
        g = jnp.einsum('ecd,efd->ecf', xin, gw) + gb[:, None, :]
        eo = jax.nn.silu(g) * up
        eo = jnp.einsum('ecf,edf->ecd', eo, down_w) + down_b[:, None, :]
        flat = (eo * topk_score[..., None]).reshape(-1, Dm)
        out = jnp.zeros_like(h).at[topk_ids.reshape(-1)].add(flat)
        out = out.reshape(B, S, Dm)
        shared = jax.nn.silu(jnp.einsum('bsd,fd->bsf', x, sh_gate_w)) * jnp.einsum('bsd,fd->bsf', x, sh_up_w)
        shared = jnp.einsum('bsf,df->bsd', shared, sh_down_w)
        return out + shared
    x = x + jnp.tanh(g_xattn[0]) * _L0_xattn_ref(_layernorm(x, axis=-1), ctx_1024, ctx_1024, L0_xattn_w, L0_xattn_u)
    x = x + jnp.tanh(g_ffn[0]) * _L0_ffn_ref(_layernorm(x, axis=-1), L0_ffn_gate_w, L0_ffn_up_w, L0_ffn_up_b, L0_ffn_gw, L0_ffn_gb, L0_ffn_down_w, L0_ffn_down_b, L0_ffn_sh_gate_w, L0_ffn_sh_up_w, L0_ffn_sh_down_w)
    return x

_drawn_inputs = setup_inputs


def setup_inputs(seed=0):
    import zlib

    import numpy as np

    out = dict(_drawn_inputs(seed))
    spreads = {}
    factors = {}
    for name, (base, spread) in spreads.items():
        noise = np.random.default_rng([zlib.crc32(name.encode()), seed]).standard_normal(out[name].shape)
        drawn = base * np.exp(spread * noise) if base else spread * noise
        out[name] = jnp.asarray(drawn.astype(out[name].dtype))
    for name, factor in factors.items():
        out[name] = (out[name] * factor).astype(out[name].dtype)
    return out
```

```python
import concourse.bass as bass
from concourse import mybir
from contextlib import ExitStack


def flamingo_layer(nc, x_in, ctx_in, wu_in, g_in, gatew_in, shgu_in, shd_in, gu_in, dn_in, fb_in, db_in, out):
    f32, f32r, bf16, fp16 = mybir.dt.float32, mybir.dt.float32r, mybir.dt.bfloat16, mybir.dt.float16
    i32, u32 = mybir.dt.int32, mybir.dt.uint32
    ALU, ACT, AX = mybir.AluOpType, mybir.ActivationFunctionType, mybir.AxisListType

    P = 128
    B, T, C = 8, 256, 256
    H = C // P
    NT = B * T // P
    NE, F, SH = 16, 1024, 512
    CAP = B * T // NE * 2
    SEG = T + 1
    L = H * SEG + 1
    ROW = C + NE
    FT = F // P
    ST = SH // P
    PC = 512
    GUP, DNP = FT, FT * C // PC
    NP = GUP + DNP
    CT = 512
    NCH = B * T // CT
    TPC = CT // P
    STEPS = 32
    SPC = STEPS // NCH
    EPS = 1e-5
    TOP = 16.635532
    BOTTOM = -89.0
    LO0, W0 = -96.0, 64.0

    rows = nc.dram_tensor("h_rows", (B * T, ROW), f32, kind="Internal").ap()
    out_rows = out.rearrange("b t d -> (b t) d")

    with ExitStack() as ctx:
        def sb(name, shape, dt=f32):
            return ctx.enter_context(nc.sbuf_tensor(name, shape, dt))

        def sem(name):
            return ctx.enter_context(nc.semaphore(name))

        X = sb("X", [P, NT, C])
        WH = sb("WH", [P, NP, PC], f32r)
        WL = sb("WL", [P, NP, PC], f32r)
        RAWA = sb("RAWA", [P, 4 * PC])
        RAWB = sb("RAWB", [P, 4 * PC])
        RAWD = sb("RAWD", [P, 4 * PC])
        AH = sb("AH", [P, FT * CAP], f32r)
        AL = sb("AL", [P, FT * CAP], f32r)
        HTH = sb("HTH", [P, H, B * T], f32r)
        HTL = sb("HTL", [P, H, B * T], f32r)
        XTH = sb("XTH", [P, H, CAP], f32r)
        XTL = sb("XTL", [P, H, CAP], f32r)
        GSTRIP = P - NE
        GWH = sb("GWH", [P, H, GSTRIP + P], f32r)
        GWL = sb("GWL", [P, H, GSTRIP + P], f32r)
        GW = sb("GW", [P, H, GSTRIP + P])
        ident = sb("ident", [P, P])
        identg = sb("identg", [P, P])
        diag = sb("diag", [P, H, P])
        diagg = sb("diagg", [P, H, P])
        WU = sb("WU", [P, 2 * H])
        EWU = sb("EWU", [P, 2 * H])
        GIN = sb("GIN", [P, 2])
        TG = sb("TG", [P, 2])
        eps = sb("eps", [P, 1])
        D = sb("D", [P, L])
        KB = [sb(f"KB{s}", [P, H, T]) for s in range(4)]
        HB = [sb(f"HB{s}", [P, 2, C]) for s in range(2)]
        MV1 = sb("MV1", [P, NT, 2])
        NR1 = sb("NR1", [P, NT])
        BI1 = sb("BI1", [P, NT])
        R1 = sb("R1", [P, NT])
        MV2 = sb("MV2", [P, NT, 2])
        BS = sb("BS", [P, 2 * NT, 6])
        R2 = sb("R2", [P, NT])
        T2 = sb("T2", [P, NT])
        NB2 = sb("NB2", [P, NT])
        same = sb("same", [P, P], bf16)
        before = sb("before", [P, P], bf16)
        own_block = sb("own_block", [P, P])
        spread = sb("spread", [P, P], fp16)
        bitmat, blockmat, rowmat = (KB[n][:, 0, 0:P].bitcast(i32) for n in range(3))
        colnum = sb("colnum", [P, 1], i32)
        colf = sb("colf", [P, 1])
        iota16 = sb("iota16", [P, 16])
        pick = sb("pick", [P, 2, 8])
        tid = sb("tid", [P, NT])
        IDXALL = sb("IDXALL", [P, NE, 2], u32)
        IDX = [sb(f"IDX{s}", [P, 2], u32) for s in range(2)]
        SIX = [sb(f"SIX{s}", [P, 2], u32) for s in range(2)]
        SCC = [sb(f"SCC{s}", [P, 2]) for s in range(2)]
        FB = [sb(f"FB{s}", [P, 2 * FT]) for s in range(2)]
        small = sb("small", [P, 16])
        cntb = sb("cntb", [P, 4], bf16)

        ARENA = 2 * 6 * L + 8 * 512
        AR = sb("AR", [P, ARENA])
        top = [0]

        def view(n, at=None):
            a = top[0] if at is None else at
            if at is None:
                top[0] += n
            assert a + n <= ARENA
            return AR[:, a:a + n]
        EK, KV, SA, RA, SB_, RB = [[view(L) for _ in range(2)] for _ in range(6)]
        E_, Q, RQ, TT = [[view(512) for _ in range(2)] for _ in range(4)]
        top[0] = 0
        SG = [view(512) for _ in range(2)]
        AF = [view(512) for _ in range(2)]
        KEY, MHI, MGE, PHI, PGE, SCO, TMPA, TMPB = [view(T) for _ in range(8)]
        SLT = view(NT * NE)
        SHIF, SLOF = [view(NT * NE) for _ in range(2)]
        SINT = view(NT * NE)
        SINT2 = view(NT * NE)
        SC = view(NT * NE)
        IDH = view(NE * 8).bitcast(fp16)
        IDF, IDM = PHI, PGE
        IDR = view(NE * 2)
        rest = top[0]
        OA = view(NT * NE * 8).bitcast(fp16)
        OB = view(NT * NE * 8).bitcast(fp16)
        top[0] = rest
        G = [view(2 * ROW) for _ in range(2)]
        Y = [view(2 * C) for _ in range(2)]
        DB = [view(C) for _ in range(2)]

        PS = [ctx.enter_context(nc.psum_tensor(f"PS{i}", [P, 512], f32)) for i in range(8)]
        NUM, DEN, TR, LG = PS[0:2], PS[2:4], PS[4:6], PS[6]
        OUT = PS[4:6]
        CNT = PS[7]

        consts_in = sem("consts_in")
        ctx_arrived = [sem(f"ctx_arrived{b}") for b in range(B)]
        x_arrived = [sem(f"x_arrived{b}") for b in range(B)]
        gw_arrived = sem("gw_arrived")
        rawa_arrived, rawb_arrived, rawd_arrived = sem("rawa_arrived"), sem("rawb_arrived"), sem("rawd_arrived")
        fb_arrived = [sem(f"fb_arrived{s}") for s in range(2)]
        db_arrived = [sem(f"db_arrived{s}") for s in range(2)]
        h_stored = [sem(f"h_stored{s}") for s in range(2)]
        scores_stored = sem("scores_stored")
        out_stored = sem("out_stored")
        pool_consts, routing_consts = sem("pool_consts"), sem("routing_consts")
        gates_exp = sem("gates_exp")
        dve_consts = sem("dve_consts")
        ln1_stats, ln1_rstd, ln1_affine = sem("ln1_stats"), sem("ln1_rstd"), sem("ln1_affine")
        act_order, dve_order, pool_order = sem("act_order"), sem("dve_order"), sem("pool_order")
        ek_ready, kv_ready, scans_done, comb_done = sem("ek_ready"), sem("kv_ready"), sem("scans_done"), sem("comb_done")
        e_ready, q_ready, rq_ready, t_ready, x1_ready = sem("e_ready"), sem("q_ready"), sem("rq_ready"), sem("t_ready"), sem("x1_ready")
        ln2_stats, ln2_rstd, ln2_affine = sem("ln2_stats"), sem("ln2_rstd"), sem("ln2_affine")
        h_ready, ht_ready, hthi_ready, htlo_ready = sem("h_ready"), sem("ht_ready"), sem("hthi_ready"), sem("htlo_ready")
        logits_done = sem("logits_done")
        w_hi, w_lo, wd_lo = sem("w_hi"), sem("w_lo"), sem("wd_lo")
        key_ready, scores_ready, scores_turned, scores_laid = sem("key_ready"), sem("scores_ready"), sem("scores_turned"), sem("scores_laid")
        counted, totals = sem("counted"), sem("totals")
        step_order = sem("step_order")
        gu_done, silu_done, gu_free = sem("gu_done"), sem("silu_done"), sem("gu_free")
        acthi_done, actlo_done, act_used = sem("acthi_done"), sem("actlo_done"), sem("act_used")
        down_read = sem("down_read")
        slots_turned, slots_ready, onehots, ids_done, idx_ready = sem("slots_turned"), sem("slots_ready"), sem("onehots"), sem("ids_done"), sem("idx_ready")
        ids_masked, ids_spread = sem("ids_masked"), sem("ids_spread")
        tails, tail_tot = sem("tails"), sem("tail_tot")
        rows_gathered = [sem(f"rows_gathered{s}") for s in range(2)]
        xt_turned, xthi_done, xtlo_done = sem("xt_turned"), sem("xthi_done"), sem("xtlo_done")
        y_biased, y_ready, scattered = sem("y_biased"), sem("y_ready"), sem("scattered")
        idx_copied = sem("idx_copied")
        kept, rows_known = sem("kept"), sem("rows_known")

        NCONST = 2
        ctx_v = ctx_in
        block = ctx.enter_context(nc.Block())

        SN = NCH * ST
        SPIECES = ST + ST * C // PC
        SBASE = GUP - 2

        def pick_expert(ap, e):
            if isinstance(e, int):
                return ap[e]
            return ap[bass.ds(e, 1), :, :].rearrange("o p n -> (o p) n")

        def tokens(t):
            return t[:, 1:1 + H * SEG].rearrange("p (h t) -> p h t", h=H)[:, :, 0:T]

        @block.sync
        def _(sp):
            sp.dma_start(WU[:], wu_in).then_inc(consts_in, 16)
            sp.dma_start(GIN[:], g_in).then_inc(consts_in, 16)

            def load_batch(b):
                if b >= 4:
                    sp.wait_ge(kv_ready, b - 3)
                sp.dma_start(KB[b % 4][:], ctx_in[:, b, :, :]).then_inc(ctx_arrived[b], 16)
                sp.dma_start(X[:, 2 * b:2 * b + 2, :], x_in[b].rearrange("(i p) d -> p i d", p=P)).then_inc(x_arrived[b], 16)
            for b in range(4):
                load_batch(b)
            sp.dma_start(RAWA[:], shgu_in).then_inc(rawa_arrived, 16)
            sp.dma_start(RAWB[:, 0:ST * C], shd_in).then_inc(rawb_arrived, 16)
            sp.wait_ge(dve_consts, 1)
            sp.dma_start(GW[:, :, GSTRIP:GSTRIP + NE], gatew_in).then_inc(gw_arrived, 16)
            for b in range(4, B):
                load_batch(b)
            sp.dma_start(RAWD[:], dn_in[0]).then_inc(rawd_arrived, 16)
            for b in range(B):
                sp.wait_ge(h_ready, 2 * (b + 1))
                sp.dma_start(rows[b * T:(b + 1) * T, 0:C].rearrange("(i p) d -> p i d", p=P), HB[b % 2][:]).then_inc(h_stored[b % 2], 16)
            sp.wait_ge(w_lo, ST)
            sp.dma_start(RAWA[:], gu_in[0, :, 0:4 * PC]).then_inc(rawa_arrived, 16)
            sp.wait_ge(w_lo, SPIECES)
            sp.dma_start(RAWB[:], gu_in[0, :, 4 * PC:8 * PC]).then_inc(rawb_arrived, 16)
            sp.dma_start(FB[0][:], fb_in[0]).then_inc(fb_arrived[0], 16)
            sp.wait_ge(scores_laid, 2)
            sp.dma_start(rows[:, C:ROW].rearrange("(i p) e -> p i e", p=P), SC.rearrange("p (i e) -> p i e", e=NE)).then_inc(scores_stored, 16)
            with sp.Fori(0, NCH) as c:
                sp.wait_ge(down_read, TPC * c + 2 * TPC)
                sp.dma_start(out_rows.rearrange("(c i p) d -> c p i d", p=P, i=TPC)[bass.ds(c, 1), :, :, :].rearrange("o p i d -> (o p) i d"),
                             X[:, bass.ds(c * TPC, TPC), :]).then_inc(out_stored, 16)
            sp.wait_ge(idx_ready, 1)
            sp.dma_start(DB[0][:], db_in[0:1, :].rearrange("o d -> (o d)").partition_broadcast(P)).then_inc(db_arrived[0], 16)

            def load_expert(e, s, first=False):
                done = SPIECES + GUP * (e - 1)
                sp.wait_ge(w_lo, done + 4)
                sp.dma_start(RAWA[:], pick_expert(gu_in, e)[:, 0:4 * PC]).then_inc(rawa_arrived, 16)
                sp.wait_ge(w_lo, done + 8)
                sp.dma_start(RAWB[:], pick_expert(gu_in, e)[:, 4 * PC:8 * PC]).then_inc(rawb_arrived, 16)
                sp.wait_ge(wd_lo, DNP * e)
                sp.dma_start(RAWD[:], pick_expert(dn_in, e)).then_inc(rawd_arrived, 16)
                if not first:
                    sp.wait_ge(y_biased, 2 * (e - 1))
                sp.dma_start(FB[s][:], pick_expert(fb_in, e)).then_inc(fb_arrived[s], 16)
                sp.dma_start(DB[s][:], (db_in[e:e + 1, :] if isinstance(e, int) else db_in[bass.ds(e, 1), :])
                             .rearrange("o d -> (o d)").partition_broadcast(P)).then_inc(db_arrived[s], 16)

            load_expert(1, 1, first=True)
            with sp.Fori(0, (NE - 2) // 2) as pair:
                for s in range(2):
                    load_expert(pair * 2 + (s + 2), s)
            sp.wait_ge(out_stored, 16 * NCH)
            sp.wait_ge(scattered, 32 * NE)
            sp.wait_ge(scores_stored, 16)
            for s in range(2):
                sp.wait_ge(h_stored[s], 16 * B // 2)

        @block.gpsimd
        def _(pool):
            nc.gpsimd.memset(ident[:], 0.0).then_inc(pool_order, 1)
            pool.wait_ge(pool_order, 1)
            nc.gpsimd.affine_select(out=ident[:], in_=ident[:], compare_op=ALU.not_equal, fill=1.0, base=0,
                                    pattern=[[-1, P]], channel_multiplier=1).then_inc(pool_consts, 1)
            n = [1]

            def mark(ins):
                n[0] += 1
                ins.then_inc(pool_order, 1)

            nc.gpsimd.iota(iota16[:], pattern=[[1, 16]], base=0, channel_multiplier=0,
                           allow_small_or_imprecise_dtypes=True).then_inc(pool_consts, 1)
            nc.gpsimd.iota(tid[:], pattern=[[P, NT]], base=0, channel_multiplier=1,
                           allow_small_or_imprecise_dtypes=True).then_inc(pool_consts, 1)
            nc.gpsimd.iota(small[:, 8:16].bitcast(i32), pattern=[[1, 8]], base=P, channel_multiplier=-1).then_inc(pool_consts, 1)
            nc.gpsimd.iota(colnum[:], pattern=[[0, 1]], base=0, channel_multiplier=1).then_inc(pool_consts, 1)
            for s in range(2):
                for t in (EK[s], KV[s]):
                    mark(nc.gpsimd.memset(t[:, 0:L:SEG], 0.0))
            pads = n[0]

            def product(b):
                pool.wait_ge(pool_order, pads)
                pool.wait_ge(ek_ready, b + 1)
                nc.gpsimd.tensor_tensor(tokens(KV[b % 2]), tokens(EK[b % 2]), KB[b % 4][:], ALU.mult).then_inc(kv_ready, 1)

            product(0)
            for i in range(B + 3):
                if i + 1 < B:
                    product(i + 1)
                b = i - 2
                if 0 <= b < B:
                    pool.wait_ge(t_ready, b + 1)
                    pool.wait_ge(x_arrived[b], 16)
                    nc.gpsimd.tensor_tensor(X[:, 2 * b:2 * b + 2, :], X[:, 2 * b:2 * b + 2, :],
                                            TT[b % 2].rearrange("p (i c) -> p i c", i=2), ALU.add).then_inc(x1_ready, 1)

            nc.gpsimd.iota(bitmat, pattern=[[-1, P]], base=256, channel_multiplier=1).then_inc(routing_consts, 1)
            nc.gpsimd.iota(blockmat, pattern=[[16, 8], [0, 16]], base=15, channel_multiplier=-1).then_inc(routing_consts, 1)
            nc.gpsimd.iota(rowmat, pattern=[[1, P]], base=0, channel_multiplier=0).then_inc(routing_consts, 1)

            def wait_all(*waits):
                counts = [v if isinstance(v, int) else pool.to_reg(v) for _, v in waits]
                pool.wait_ge(pool_consts, 5)
                for (signal, _), count in zip(waits, counts):
                    pool.wait_ge(signal, count)

            with pool.Fori(0, NCH) as c:
                for ft in range(ST):
                    wait_all((gu_free, c * ST + (ft + 3)), (act_used, c * ST + (ft + 1)))
                    nc.gpsimd.tensor_scalar(AH[:, ft * CT:(ft + 1) * CT], AF[ft % 2], 1.0, 0.0, ALU.mult, ALU.add).then_inc(acthi_done, 1)
            pool.wait_ge(act_used, ST + SN)

            def fetch(e, s):
                nc.gpsimd.tensor_copy(IDX[s][:], index_of(e)).then_inc(idx_copied, 1)
                wait_all((idx_copied, e + 1))
                for j in range(2):
                    pool.indirect_dma_start(G[s][:, j * ROW:(j + 1) * ROW], None, rows,
                                            bass.IndirectOffsetOnAxis(ap=IDX[s][:, j:j + 1], axis=0)).then_inc(rows_gathered[s], 16)

            def index_of(e):
                return IDXALL[:, e, :] if isinstance(e, int) else IDXALL[:, bass.ds(e, 1), :].rearrange("p o j -> p (o j)")

            def keep_scores(e, s):
                sc = G[s][:, C + e:C + e + ROW + 1:ROW] if isinstance(e, int) else G[s][:, bass.ds(e + C, 2, step=ROW)]
                wait_all((rows_gathered[s], 16 * (e - s) + 32))
                nc.gpsimd.tensor_copy(SCC[s][:], sc).then_inc(kept, 1)

            def finish(e, s):
                before_it = (out_stored, 16 * NCH) if isinstance(e, int) and e == 0 else (scattered, 32 * e)
                wait_all(before_it)
                nc.gpsimd.tensor_copy(SIX[s][:], index_of(e)).then_inc(rows_known, 1)
                for j in range(2):
                    wait_all((kept, e + 1), (y_biased, 2 * e + (j + 1)))
                    nc.gpsimd.tensor_scalar(Y[s][:, j * C:(j + 1) * C], Y[s][:, j * C:(j + 1) * C],
                                            SCC[s][:, j:j + 1], TG[:, 1:2], ALU.mult, ALU.mult).then_inc(y_ready, 1)
                wait_all((y_ready, 2 * e + 2), (rows_known, e + 1))
                for j in range(2):
                    pool.indirect_dma_start(out_rows, bass.IndirectOffsetOnAxis(ap=SIX[s][:, j:j + 1], axis=0),
                                            Y[s][:, j * C:(j + 1) * C], None, compute_op=ALU.add).then_inc(scattered, 16)

            def down_lo(e, q):
                wait_all((w_hi, SPIECES + NP * e + (GUP + q + 1)))
                nc.gpsimd.tensor_tensor(WL[:, GUP + q, :], RAWD[:, q * PC:(q + 1) * PC],
                                        WH[:, GUP + q, :].bitcast(f32), ALU.subtract).then_inc(wd_lo, 1)

            def expert(e, s, first=False, last=False):
                keep_scores(e, s)
                if not last:
                    fetch(e + 1, 1 - s)
                if not first:
                    finish(e - 1, 1 - s)
                if not last:
                    for q in range(DNP):
                        down_lo(e + 1, q)

            pool.wait_ge(idx_ready, 1)
            pool.wait_ge(scores_stored, 16)
            for s in range(2):
                pool.wait_ge(h_stored[s], 16 * B // 2)
            fetch(0, 0)
            for q in range(DNP):
                down_lo(0, q)
            expert(0, 0, first=True)
            with pool.Fori(0, (NE - 2) // 2) as pair:
                for s in range(2):
                    expert(pair * 2 + (s + 1), 1 - s)
            expert(NE - 1, 1, last=True)
            finish(NE - 1, 1)

        @block.scalar
        def _(act):
            n = [0]

            def link(ins):
                n[0] += 1
                ins.then_inc(act_order, 1)
                act.wait_ge(act_order, n[0])

            act.wait_ge(consts_in, 16 * NCONST)
            act.wait_ge(dve_consts, 1)
            nc.scalar.activation(TG[:], GIN[:], ACT.Tanh).then_inc(gates_exp, 1)
            nc.scalar.preload_act_table_set("natural_log_exp_and_others")
            nc.scalar.activation(EWU[:], WU[:], ACT.Exp).then_inc(gates_exp, 1)

            def exp_k(b):
                act.wait_ge(ctx_arrived[b], 16)
                if b >= 2:
                    act.wait_ge(comb_done, b - 1)
                else:
                    act.wait_ge(pool_order, 5)
                nc.scalar.activation(tokens(EK[b % 2]), KB[b % 4][:], ACT.Exp).then_inc(ek_ready, 1)

            def ln1(g):
                act.wait_ge(ln1_stats, g + 1)
                a = slice(8 * g, 8 * g + 8)
                link(nc.scalar.activation(R1[:, a], MV1[:, a, 1], ACT.Ln, bias=eps[:, 0:1]))
                nc.scalar.activation(R1[:, a], R1[:, a], ACT.Exp, scale=-0.5).then_inc(ln1_rstd, 1)

            exp_k(0)
            ln1(0)
            for i in range(B + 4):
                b = i - 4
                if 0 <= b < B:
                    act.wait_ge(ht_ready, b + 1)
                    nc.scalar.activation(HTH[:, :, b * T:(b + 1) * T], TR[b % 2][:].rearrange("p (k t) -> p k t", k=H),
                                         ACT.Copy).then_inc(hthi_ready, 1)
                b = i - 3
                if 0 <= b < B:
                    act.wait_ge(ln2_affine, b + 1)
                    if b >= 2:
                        act.wait_ge(ht_ready, b - 1)
                        act.wait_ge(h_stored[b % 2], 16 * (b // 2))
                    for j in range(2):
                        t = 2 * b + j
                        nc.scalar.activation(HB[b % 2][:, j, :], X[:, t, :], ACT.Identity, scale=R2[:, t:t + 1],
                                             bias=NB2[:, t:t + 1]).then_inc(h_ready, 1)
                if i + 1 < B:
                    exp_k(i + 1)
                if i == 3:
                    ln1(1)
                b = i
                if b < B:
                    act.wait_ge(ln1_affine, 1 + b // 4)
                    if b >= 2:
                        act.wait_ge(q_ready, b - 1)
                    for j in range(2):
                        t = 2 * b + j
                        nc.scalar.activation(E_[b % 2][:, j * C:(j + 1) * C], X[:, t, :], ACT.Exp, scale=NR1[:, t:t + 1],
                                             bias=BI1[:, t:t + 1]).then_inc(e_ready, 1)
                b = i - 1
                if 0 <= b < B:
                    act.wait_ge(q_ready, b + 1)
                    link(nc.scalar.activation(Q[b % 2], Q[b % 2], ACT.Ln))
                    if b >= 2:
                        act.wait_ge(t_ready, b - 1)
                    nc.scalar.activation(RQ[b % 2], Q[b % 2], ACT.Exp, scale=-1.0).then_inc(rq_ready, 1)
                b = i - 2
                if 0 <= b < B:
                    act.wait_ge(ln2_stats, b + 1)
                    a = slice(2 * b, 2 * b + 2)
                    link(nc.scalar.activation(R2[:, a], MV2[:, a, 1], ACT.Ln, bias=eps[:, 0:1]))
                    nc.scalar.activation(R2[:, a], R2[:, a], ACT.Exp, scale=-0.5).then_inc(ln2_rstd, 1)

            def hi_weight(n, piece, raw):
                nc.scalar.activation(WH[:, piece, :], raw, ACT.Copy).then_inc(w_hi, 1)

            def raw_of(piece):
                return (RAWA, RAWB, RAWD)[piece // 4][:, piece % 4 * PC:(piece % 4 + 1) * PC]

            act.wait_ge(rawa_arrived, 16)
            act.wait_ge(rawb_arrived, 16)
            for q in range(SPIECES):
                hi_weight(q, SBASE + q, (RAWA[:, q * PC:(q + 1) * PC] if q < ST else RAWB[:, (q - ST) * PC:(q - ST + 1) * PC]))

            act.wait_ge(key_ready, 1)
            nc.scalar.activation(SCO, LG[:, 0:T], ACT.Sigmoid).then_inc(scores_ready, 1)
            for j in range(2):
                act.wait_ge(scores_turned, 2)
                nc.scalar.activation(SC.rearrange("p (b j e) -> p b j e", j=2, e=NE)[:, :, j, :],
                                     PS[7][:, j * P:(j + 1) * P].rearrange("p (b e) -> p b e", e=NE), ACT.Copy).then_inc(scores_laid, 1)

            with act.Fori(0, NCH) as c:
                for ft in range(ST):
                    act.wait_ge(gu_done, c * ST + (ft + 1))
                    act.wait_ge(gu_free, c * ST + (ft + 1))
                    nc.scalar.activation(SG[ft % 2], PS[ft % 2][:], ACT.Silu).then_inc(silu_done, 1)

            act.wait_ge(rawa_arrived, 32)
            act.wait_ge(rawb_arrived, 32)
            for q in range(GUP):
                if q == SBASE:
                    act.wait_ge(act_used, ST + SN)
                hi_weight(q, q, raw_of(q))
            act.wait_ge(rawd_arrived, 16)
            for q in range(GUP, NP):
                hi_weight(q, q, raw_of(q))

            def xt_hi(e):
                act.wait_ge(xt_turned, e + 1)
                nc.scalar.activation(XTH[:], PS[6][:].rearrange("p (k t) -> p k t", k=H), ACT.Copy).then_inc(xthi_done, 1)

            xt_hi(0)

            def expert(e, s, last=False):
                act.wait_ge(fb_arrived[s], 8 * (e - s) + 16)
                for f in range(FT):
                    act.wait_ge(gu_done, SN + FT * e + (f + 1))
                    act.wait_ge(gu_free, SN + FT * e + (f + 1))
                    nc.scalar.activation(SG[f % 2][:, 0:CAP], PS[f % 4][:, 0:CAP], ACT.Silu, bias=FB[s][:, f:f + 1]).then_inc(silu_done, 1)
                    if f >= 1:
                        hi_of(e, f - 1)
                        if not last:
                            next_hi(e, f - 1)
                hi_of(e, FT - 1)
                if last:
                    return
                next_hi(e, GUP - 1)
                next_hi(e, GUP)
                xt_hi(e + 1)
                for q in range(GUP + 1, NP):
                    next_hi(e, q)

            def hi_of(e, f):
                act.wait_ge(gu_free, SN + FT * e + (f + 3))
                act.wait_ge(act_used, SN + FT * e + (f + 1 - FT + ST))
                nc.scalar.activation(AH[:, f * CAP:(f + 1) * CAP], AF[f % 2][:, 0:CAP], ACT.Copy).then_inc(acthi_done, 1)

            def next_hi(e, q):
                if q % 4 == 0:
                    if q < GUP:
                        act.wait_ge((rawa_arrived, rawb_arrived)[q // 4], 16 * e + 48)
                    else:
                        act.wait_ge(rawd_arrived, 16 * e + 32)
                if q < GUP:
                    act.wait_ge(gu_done, SN + FT * e + (q + 1))
                else:
                    act.wait_ge(act_used, ST + SN + FT * e + 2 * (q - GUP + 1))
                hi_weight(q, q, raw_of(q))

            expert(0, 0)
            with act.Fori(0, (NE - 2) // 2) as pair:
                for s in range(2):
                    expert(pair * 2 + (s + 1), 1 - s)
            expert(NE - 1, 1, last=True)

        @block.vector
        def _(dve):
            n = [0]

            def mark(ins):
                n[0] += 1
                ins.then_inc(dve_order, 1)

            def link(ins):
                mark(ins)
                dve.wait_ge(dve_order, n[0])

            V = nc.vector
            mark(V.memset(D[:], 1.0))
            mark(V.memset(eps[:], EPS))
            link(V.memset(GW[:], 0.0))
            V.memset(small[:, 0:1], LO0).then_inc(dve_consts, 1)
            dve.wait_ge(dve_consts, 1)
            dve.wait_ge(gates_exp, 2)
            for h in range(H):
                mark(V.tensor_scalar(D[:, h * SEG + 1:(h + 1) * SEG], D[:, h * SEG + 1:(h + 1) * SEG], EWU[:, h:h + 1], None, ALU.mult))
            link(V.memset(D[:, 0:L:SEG], 0.0))

            def ln1(g):
                for t in range(8 * g, 8 * g + 8):
                    dve.wait_ge(x_arrived[t // 2], 16)
                    mark(V.bn_stats(BS[:, t, :], X[:, t, :]))
                dve.wait_ge(dve_order, n[0])
                for t in range(8 * g, 8 * g + 8):
                    ins = V.bn_aggr(MV1[:, t, :], BS[:, t, :])
                    if t < 8 * g + 7:
                        mark(ins)
                    else:
                        ins.then_inc(ln1_stats, 1)

            def ln1_scale(g):
                a = slice(8 * g, 8 * g + 8)
                dve.wait_ge(ln1_rstd, g + 1)
                mark(V.tensor_scalar(NR1[:, a], R1[:, a], -1.0, None, ALU.mult))
                V.tensor_tensor(BI1[:, a], MV1[:, a, 0], R1[:, a], ALU.mult).then_inc(ln1_affine, 1)

            dve.wait_ge(pool_consts, 5)
            mark(V.tensor_scalar(identg[:], ident[:], TG[:, 0:1], None, ALU.mult))
            for h in range(H):
                mark(V.tensor_scalar(diag[:, h, :], ident[:], EWU[:, H + h:H + h + 1], None, ALU.mult))
            dve.wait_ge(dve_order, n[0])
            for h in range(H):
                V.tensor_scalar(diagg[:, h, :], diag[:, h, :], TG[:, 0:1], None, ALU.mult).then_inc(dve_consts, 1)
            ln1(0)

            def split_weight(count, piece, raw):
                dve.wait_ge(w_hi, count)
                V.tensor_tensor(WL[:, piece, :], raw, WH[:, piece, :].bitcast(f32), ALU.subtract).then_inc(w_lo, 1)

            for i in range(B + 4):
                b = i - 3
                if 0 <= b < B:
                    a = slice(2 * b, 2 * b + 2)
                    dve.wait_ge(ln2_rstd, b + 1)
                    link(V.tensor_tensor(T2[:, a], R2[:, a], R2[:, a], ALU.mult))
                    link(V.scalar_tensor_tensor(T2[:, a], MV2[:, a, 1], EPS, T2[:, a], ALU.add, ALU.mult))
                    link(V.tensor_scalar(T2[:, a], T2[:, a], -0.5, 1.5, ALU.mult, ALU.add))
                    link(V.tensor_tensor(R2[:, a], R2[:, a], T2[:, a], ALU.mult))
                    V.scalar_tensor_tensor(NB2[:, a], MV2[:, a, 0], -1.0, R2[:, a], ALU.mult, ALU.mult).then_inc(ln2_affine, 1)
                b = i - 2
                if 0 <= b < B:
                    dve.wait_ge(rq_ready, b + 1)
                    if b >= 2:
                        dve.wait_ge(x1_ready, b - 1)
                    V.tensor_tensor(TT[b % 2], NUM[b % 2][:], RQ[b % 2], ALU.mult).then_inc(t_ready, 1)
                b = i
                if b < B:
                    s = b % 2
                    if i == 0:
                        dve.wait_ge(dve_order, n[0])
                    if b >= 2:
                        dve.wait_ge(comb_done, b - 1)
                    dve.wait_ge(ek_ready, b + 1)
                    for src, fw, bw in ((EK[s], SB_[s], RB[s]), (KV[s], SA[s], RA[s])):
                        if src is KV[s]:
                            dve.wait_ge(kv_ready, b + 1)
                        V.tensor_tensor_scan(fw, D[:], src, 0.0, ALU.mult, ALU.add).then_inc(scans_done, 1)
                        V.tensor_tensor_scan(bw[:, ::-1], D[:, ::-1], src[:, ::-1], 0.0, ALU.mult, ALU.add).then_inc(scans_done, 1)
                if i == 0:
                    ln1_scale(0)
                if i == 2:
                    ln1(1)
                if i == 3:
                    ln1_scale(1)
                b = i - 1
                if 0 <= b < B:
                    dve.wait_ge(comb_done, b + 1)
                    dve.wait_ge(e_ready, 2 * b + 2)
                    if b >= 2:
                        dve.wait_ge(rq_ready, b - 1)
                    V.scalar_tensor_tensor(Q[b % 2], E_[b % 2], 1.0, DEN[b % 2][:], ALU.add, ALU.mult).then_inc(q_ready, 1)
                b = i - 2
                if 0 <= b < B:
                    dve.wait_ge(x1_ready, b + 1)
                    for j in range(2):
                        mark(V.bn_stats(BS[:, NT + 2 * b + j, :], X[:, 2 * b + j, :]))
                    dve.wait_ge(dve_order, n[0])
                    mark(V.bn_aggr(MV2[:, 2 * b, :], BS[:, NT + 2 * b, :]))
                    V.bn_aggr(MV2[:, 2 * b + 1, :], BS[:, NT + 2 * b + 1, :]).then_inc(ln2_stats, 1)
                    if b == 0:
                        dve.wait_ge(gw_arrived, 16)
                        link(V.tensor_copy(GWH[:], GW[:]))
                        mark(V.tensor_tensor(GWL[:], GW[:], GWH[:].bitcast(f32), ALU.subtract))
                b = i - 4
                if 0 <= b < B:
                    dve.wait_ge(hthi_ready, b + 1)
                    V.tensor_tensor(HTL[:, :, b * T:(b + 1) * T], TR[b % 2][:].rearrange("p (k t) -> p k t", k=H),
                                    HTH[:, :, b * T:(b + 1) * T].bitcast(f32), ALU.subtract).then_inc(htlo_ready, 1)

            for q in range(SPIECES):
                split_weight(q + 1, SBASE + q, (RAWA[:, q * PC:(q + 1) * PC] if q < ST else RAWB[:, (q - ST) * PC:(q - ST + 1) * PC]))

            dve.wait_ge(routing_consts, 3)
            link(V.tensor_scalar(TMPA[:, 0:P].bitcast(i32), bitmat, 15, None, ALU.bitwise_and))
            mark(V.tensor_scalar(same[:], TMPA[:, 0:P].bitcast(i32), 0.0, None, ALU.is_equal))
            link(V.tensor_scalar(TMPB[:, 0:P], bitmat, 256.0, None, ALU.is_lt))
            mark(V.tensor_tensor(before[:], same[:], TMPB[:, 0:P], ALU.mult))
            link(V.tensor_scalar(small[:, 8:16].bitcast(i32), small[:, 8:16].bitcast(i32), 7, None, ALU.bitwise_and))
            for j in range(2):
                mark(V.tensor_scalar(pick[:, j, :], small[:, 8:16].bitcast(i32), 0.0, None, ALU.is_equal))
            link(V.tensor_scalar(blockmat, blockmat, 4, None, ALU.arith_shift_right))
            mark(V.tensor_scalar(own_block[:], blockmat, 0.0, None, ALU.is_equal))
            mark(V.tensor_scalar(rowmat, rowmat, 3, None, ALU.arith_shift_right))
            link(V.tensor_scalar(colnum[:], colnum[:], 15, None, ALU.bitwise_and))
            link(V.tensor_copy(colf[:], colnum[:]))
            link(V.tensor_scalar(spread[:], rowmat, colf[:, 0:1], None, ALU.is_equal))
            lo, w, mid, d = (small[:, k:k + 1] for k in range(4))
            mark(V.memset(w, W0))
            link(V.memset(mid, LO0 + W0))

            dve.wait_ge(logits_done, 1)
            V.tensor_scalar(KEY, LG[:, 0:T], TOP, BOTTOM, ALU.min, ALU.max).then_inc(key_ready, 1)
            dve.wait_ge(key_ready, 1)

            def count():
                V.tensor_scalar(TMPA, KEY, mid, None, ALU.is_ge, ALU.add, accum_out=cntb[:, 0:1]).then_inc(counted, 1)

            def step(k, last=False):
                dve.wait_ge(totals, k + 1)
                V.scalar_tensor_tensor(d, CNT[:, 0:1], float(CAP), w, ALU.is_ge, ALU.mult).then_inc(step_order, 1)
                dve.wait_ge(step_order, 4 * k + 1)
                V.tensor_tensor(lo, lo, d, ALU.add).then_inc(step_order, 1)
                V.tensor_scalar(w, w, 0.5, None, ALU.mult).then_inc(step_order, 1)
                dve.wait_ge(step_order, 4 * k + 3)
                V.tensor_tensor(mid, lo, w, ALU.add).then_inc(step_order, 1)
                dve.wait_ge(step_order, 4 * k + 4)
                if not last:
                    count()

            dve.wait_ge(scores_laid, 2)
            dve.sem_inc(gu_free, 2)
            dve.sem_inc(actlo_done, 2)
            dve.sem_inc(act_used, ST)
            dve.sem_inc(down_read, TPC)
            count()

            def glu(n, sg, u, af, bias=None):
                dve.wait_ge(silu_done, n + 1)
                dve.wait_ge(actlo_done, n + 1)
                if bias is None:
                    ins = V.tensor_tensor(af, u, sg, ALU.mult)
                else:
                    ins = V.scalar_tensor_tensor(af, u, bias, sg, ALU.add, ALU.mult)
                ins.then_inc(gu_free, 1)

            def act_lo(n, af, sl):
                dve.wait_ge(acthi_done, n + 1)
                V.tensor_tensor(AL[:, sl], af, AH[:, sl].bitcast(f32), ALU.subtract).then_inc(actlo_done, 1)

            with dve.Fori(0, NCH) as c:
                def shared_glu(ft):
                    glu(c * ST + ft, SG[ft % 2], PS[2 + ft % 2][:], AF[ft % 2])

                def shared_lo(ft):
                    act_lo(c * ST + ft, AF[ft % 2], slice(ft * CT, (ft + 1) * CT))

                def shared_step(k):
                    step(c * SPC + k)
                shared_step(0)
                shared_glu(0)
                shared_step(1)
                shared_lo(0)
                shared_step(2)
                shared_glu(1)
                shared_step(3)
                shared_lo(1)
                shared_glu(2)
                shared_step(4)
                shared_lo(2)
                shared_glu(3)
                shared_step(5)
                shared_lo(3)
                shared_step(6)
                shared_step(7)
                dve.wait_ge(act_used, ST + c * ST + ST)
                for tt in range(TPC):
                    xs = X[:, bass.ds(c * TPC + tt, 1), :].rearrange("p o d -> p (o d)")
                    V.scalar_tensor_tensor(xs, OUT[tt // 2][:, tt % 2 * C:(tt % 2 + 1) * C], TG[:, 1:2], xs,
                                           ALU.mult, ALU.add).then_inc(down_read, 1)
            dve.wait_ge(totals, STEPS + 1)

            hi = mid
            c_hi, c_ge, off1, off2 = cntb[:, 1:2], cntb[:, 2:3], small[:, 4:5], small[:, 5:6]
            mark(V.tensor_scalar(MHI, KEY, lo, None, ALU.is_gt))
            link(V.tensor_scalar(TMPB, KEY, hi, None, ALU.is_ge))
            mark(V.tensor_tensor(MHI, MHI, TMPB, ALU.mult))
            link(V.tensor_scalar(MGE, KEY, lo, None, ALU.is_ge, ALU.add, accum_out=c_ge))
            mark(V.tensor_scalar(TMPA, MHI, 1.0, None, ALU.mult, ALU.add, accum_out=c_hi))
            V.memset(TMPB, 1.0).then_inc(tails, 1)
            dve.wait_ge(tails, 1)
            dve.wait_ge(dve_order, n[0])
            mark(V.tensor_tensor_scan(PHI, TMPB, MHI, 0.0, ALU.mult, ALU.add))
            mark(V.tensor_tensor_scan(PGE, TMPB, MGE, 0.0, ALU.mult, ALU.add))
            dve.wait_ge(tail_tot, 1)
            link(V.tensor_copy(small[:, 5:8], CNT[:, 0:3]))
            link(V.scalar_tensor_tensor(off1, small[:, 6:7], 1.0, small[:, 5:6], ALU.mult, ALU.subtract))
            link(V.tensor_tensor(off1, off1, small[:, 7:8], ALU.add))
            link(V.scalar_tensor_tensor(TMPA, PGE, off1, PHI, ALU.add, ALU.subtract))
            link(V.scalar_tensor_tensor(TMPB, PHI, small[:, 5:6], TMPA, ALU.add, ALU.subtract))
            mark(V.tensor_tensor(TMPB, TMPB, MHI, ALU.mult))
            link(V.tensor_tensor(TMPA, TMPA, MGE, ALU.mult))
            V.tensor_tensor(TMPA, TMPA, TMPB, ALU.add).then_inc(slots_ready, 1)
            slt = SLT.rearrange("p (b j e) -> p b j e", j=2, e=NE)
            for j in range(2):
                dve.wait_ge(slots_turned, 2)
                mark(V.tensor_copy(slt[:, :, j, :], PS[6][:, j * P:(j + 1) * P].rearrange("p (b e) -> p b e", e=NE)))
            dve.wait_ge(dve_order, n[0])
            si, si2 = SINT.bitcast(i32), SINT2.bitcast(i32)
            link(V.tensor_scalar(si, SLT, -1.0, None, ALU.add))
            mark(V.tensor_scalar(si2, si, 4, None, ALU.arith_shift_right))
            link(V.tensor_scalar(si, si, 15, None, ALU.bitwise_and))
            mark(V.tensor_copy(SHIF, si2))
            link(V.tensor_copy(SLOF, si))
            it = iota16[:].unsqueeze(1).broadcast_to([P, NT * NE, 16])
            oa = OA.rearrange("p (n s) -> p n s", s=16)
            ob = OB.rearrange("p (n s) -> p n s", s=16)
            V.tensor_tensor(oa, SHIF.unsqueeze(2).broadcast_to([P, NT * NE, 16]), it, ALU.is_equal).then_inc(onehots, 1)
            link(V.tensor_tensor(ob, SLOF.unsqueeze(2).broadcast_to([P, NT * NE, 16]), it, ALU.is_equal))
            for t in range(NT):
                a = slice(t * NE * 16, (t + 1) * NE * 16)
                V.tensor_scalar(OB[:, a], OB[:, a], tid[:, t:t + 1], None, ALU.mult).then_inc(onehots, 1)
            dve.wait_ge(ids_done, 1)
            V.tensor_tensor(IDH.rearrange("p (g e s) -> p g (e s)", g=2, s=16), PS[7][:, 0:2 * P].rearrange("p (g n) -> p g n", g=2),
                            own_block[:].unsqueeze(1).broadcast_to([P, 2, P]), ALU.mult).then_inc(ids_masked, 1)
            dve.wait_ge(ids_spread, 1)
            link(V.tensor_copy(IDF, PS[6][:, 0:NE * 16]))
            link(V.tensor_tensor(IDM.rearrange("p (e s) -> p e s", s=16), IDF.rearrange("p (e s) -> p e s", s=16),
                                 pick[:].rearrange("p j r -> p (j r)").unsqueeze(1).broadcast_to([P, NE, 16]), ALU.mult))
            link(V.tensor_reduce(IDR, IDM.rearrange("p (n r) -> p n r", r=8), AX.X, ALU.add))
            V.tensor_copy(IDXALL[:].rearrange("p e j -> p (e j)"), IDR).then_inc(idx_ready, 1)

            def raw_of(piece):
                return (RAWA, RAWB)[piece // 4][:, piece % 4 * PC:(piece % 4 + 1) * PC]

            for q in range(GUP):
                split_weight(SPIECES + q + 1, q, raw_of(q))

            def xt_lo(e):
                dve.wait_ge(xthi_done, e + 1)
                V.tensor_tensor(XTL[:], PS[6][:].rearrange("p (k t) -> p k t", k=H), XTH[:].bitcast(f32), ALU.subtract).then_inc(xtlo_done, 1)

            xt_lo(0)

            def expert(e, s, first=False, last=False):
                def next_lo(q):
                    if not last:
                        split_weight(SPIECES + NP * (e + 1) + (q + 1), q, raw_of(q))

                def lo_of(f):
                    act_lo(SN + FT * e + f, AF[f % 2][:, 0:CAP], slice(f * CAP, (f + 1) * CAP))
                for f in range(FT):
                    glu(SN + FT * e + f, SG[f % 2][:, 0:CAP], PS[f % 4][:, CAP:2 * CAP], AF[f % 2][:, 0:CAP],
                        bias=FB[s][:, FT + f:FT + f + 1])
                    if f >= 1:
                        lo_of(f - 1)
                        next_lo(f - 1)
                lo_of(FT - 1)
                next_lo(GUP - 1)
                if not last:
                    xt_lo(e + 1)
                dve.wait_ge(act_used, ST + SN + FT * e + FT)
                dve.wait_ge(db_arrived[s], 8 * (e - s) + 16)
                if not first:
                    dve.wait_ge(y_ready, 2 * e)
                for j in range(2):
                    V.tensor_tensor(Y[s][:, j * C:(j + 1) * C], OUT[j][:, 0:C], DB[s], ALU.add).then_inc(y_biased, 1)

            expert(0, 0, first=True)
            with dve.Fori(0, (NE - 2) // 2) as pair:
                for s in range(2):
                    expert(pair * 2 + (s + 1), 1 - s)
            expert(NE - 1, 1, last=True)

        @block.tensor
        def _(pe):
            M = nc.tensor.matmul

            def three(dst, lhs, rhs, start, stop, **kw):
                (lh, ll), (rh, rl) = lhs, rhs
                M(dst, lh, rh, start=start, stop=False, **kw)
                M(dst, lh, rl, start=False, stop=False, **kw)
                return M(dst, ll, rh, start=False, stop=stop, **kw)

            pe.wait_ge(dve_consts, 3)
            for i in range(B + 4):
                b = i
                if b < B:
                    s = b % 2
                    pe.wait_ge(scans_done, 4 * b + 4)
                    if b >= 2:
                        pe.wait_ge(q_ready, b - 1)
                        pe.wait_ge(t_ready, b - 1)
                    for dst, fw, own, bw, one, dg in ((DEN[s], SB_[s], EK[s], RB[s], ident[:], diag),
                                                      (NUM[s], SA[s], KV[s], RA[s], identg[:], diagg)):
                        for th in range(2):
                            for h in range(H):
                                at = h * SEG + th * P
                                o = dst[:, th * C + h * P:th * C + (h + 1) * P]
                                M(o, fw[:, at:at + P], one, start=True, stop=False)
                                M(o, bw[:, at + 2:at + 2 + P], one, start=False, stop=False)
                                last = M(o, own[:, at + 1:at + 1 + P], dg[:, h, :], start=False, stop=True)
                    last.then_inc(comb_done, 1)
                b = i - 4
                if 0 <= b < B:
                    pe.wait_ge(htlo_ready, b + 1)
                    sl = slice(b * T, (b + 1) * T)
                    win = slice(GSTRIP - NE * b, GSTRIP - NE * b + P)
                    for k in range(H):
                        last = three(LG[:, 0:T], (GWH[:, k, win], GWL[:, k, win]), (HTH[:, k, sl], HTL[:, k, sl]),
                                     start=(b == 0 and k == 0), stop=(b == B - 1 and k == H - 1))
                    if b == B - 1:
                        last.then_inc(logits_done, 1)
                b = i - 3
                if 0 <= b < B:
                    pe.wait_ge(h_ready, 2 * b + 2)
                    if b >= 2:
                        pe.wait_ge(htlo_ready, b - 1)
                    for k in range(H):
                        for th in range(2):
                            last = nc.tensor.transpose(TR[b % 2][:, k * T + th * P:k * T + (th + 1) * P],
                                                       HB[b % 2][:, th, k * P:(k + 1) * P], ident[:])
                    last.then_inc(ht_ready, 1)

            pe.wait_ge(scores_ready, 1)
            for j in range(2):
                nc.tensor.transpose(PS[7][:, j * P:(j + 1) * P], SCO[:, j * P:(j + 1) * P], ident[:]).then_inc(scores_turned, 1)

            def total(k):
                pe.wait_ge(counted, k + 1)
                M(CNT[:, 0:1], same[:], cntb[:, 0:1], start=True, stop=True).then_inc(totals, 1)

            pe.wait_ge(w_lo, SPIECES)
            pe.wait_ge(key_ready, 1)
            pe.wait_ge(htlo_ready, B)
            total_at = {("u", 0): 0, ("g", 1): 1, ("g", 2): 2, ("u", 2): 3, ("u", 3): 4, ("d", 0): 5, ("d", 2): 6, ("d", 3): 7}
            with pe.Fori(0, NCH) as c:
                for ft in range(ST):
                    piece = SBASE + ft
                    pe.wait_ge(gu_free, c * ST + (ft + 1))
                    for g, bank in ((0, ft % 2), (1, 2 + ft % 2)):
                        for k in range(H):
                            sl = slice(g * 2 * P + k * P, g * 2 * P + (k + 1) * P)
                            last = three(PS[bank][:], (WH[:, piece, sl], WL[:, piece, sl]),
                                         (HTH[:, k, bass.ds(c * CT, CT)], HTL[:, k, bass.ds(c * CT, CT)]),
                                         start=(k == 0), stop=(k == H - 1))
                        if g == 1:
                            last.then_inc(gu_done, 1)
                        if ("gu"[g], ft) in total_at:
                            total(c * SPC + total_at["gu"[g], ft])
                pe.wait_ge(down_read, c * TPC + TPC)
                for ft in range(ST):
                    pe.wait_ge(actlo_done, c * ST + (ft + 3))
                    piece, half = SBASE + ST + ft // 2, ft % 2
                    sl = slice(half * C, (half + 1) * C)
                    for tt in range(TPC):
                        a = slice(ft * CT + tt * P, ft * CT + (tt + 1) * P)
                        last = three(OUT[tt // 2][:, tt % 2 * C:(tt % 2 + 1) * C], (AH[:, a], AL[:, a]),
                                     (WH[:, piece, sl], WL[:, piece, sl]), start=(ft == 0 and tt % 2 == 0),
                                     stop=(ft == ST - 1), skip_group_check=True)
                    last.then_inc(act_used, 1)
                    if ("d", ft) in total_at:
                        total(c * SPC + total_at["d", ft])
            total(STEPS)

            pe.wait_ge(tails, 1)
            M(CNT[:, 0:2], before[:], cntb[:, 1:3], start=True, stop=True)
            M(CNT[:, 2:3], same[:], cntb[:, 1:2], start=True, stop=True).then_inc(tail_tot, 1)
            pe.wait_ge(slots_ready, 1)
            for j in range(2):
                nc.tensor.transpose(PS[6][:, j * P:(j + 1) * P], TMPA[:, j * P:(j + 1) * P], ident[:]).then_inc(slots_turned, 1)
            for t in range(NT):
                pe.wait_ge(onehots, t + 2)
                for g in range(2):
                    a = slice(t * NE * 16 + g * P, t * NE * 16 + (g + 1) * P)
                    last = M(PS[7][:, g * P:(g + 1) * P], OA[:, a], OB[:, a],
                             start=(t == 0 and g == 0), stop=(t == NT - 1), skip_group_check=True)
            last.then_inc(ids_done, 1)
            pe.wait_ge(ids_masked, 1)
            M(PS[6][:, 0:2 * P], spread[:], IDH, start=True, stop=True).then_inc(ids_spread, 1)

            def turn(e, s):
                pe.wait_ge(rows_gathered[s], 16 * (e - s) + 32)
                for k in range(H):
                    for j in range(2):
                        last = nc.tensor.transpose(PS[6][:, k * CAP + j * P:k * CAP + (j + 1) * P],
                                                   G[s][:, j * ROW + k * P:j * ROW + (k + 1) * P], ident[:])
                last.then_inc(xt_turned, 1)

            turn(0, 0)
            pe.wait_ge(gu_free, SN + 2)

            def expert(e, s, first=False, last_one=False):
                pe.wait_ge(xtlo_done, e + 1)
                for f in range(FT):
                    pe.wait_ge(w_lo, SPIECES + GUP * e + (f + 1))
                    pe.wait_ge(gu_free, SN + FT * e + (f - 1))
                    for g in range(2):
                        for k in range(H):
                            sl = slice(g * 2 * P + k * P, g * 2 * P + (k + 1) * P)
                            last = three(PS[f % 4][:, g * CAP:(g + 1) * CAP], (WH[:, f, sl], WL[:, f, sl]),
                                         (XTH[:, k, :], XTL[:, k, :]), start=(k == 0), stop=(k == H - 1))
                    last.then_inc(gu_done, 1)
                if first:
                    pe.wait_ge(down_read, TPC + NCH * TPC)
                else:
                    pe.wait_ge(y_biased, 2 * e)
                for k in range(FT):
                    if k == 2 and not last_one:
                        turn(e + 1, 1 - s)
                    pe.wait_ge(actlo_done, SN + FT * e + (k + 3))
                    if k % 2 == 0:
                        pe.wait_ge(wd_lo, DNP * e + (k // 2 + 1))
                    piece, sl = GUP + k // 2, slice(k % 2 * C, (k % 2 + 1) * C)
                    for j in range(2):
                        a = slice(k * CAP + j * P, k * CAP + (j + 1) * P)
                        last = three(OUT[j][:, 0:C], (AH[:, a], AL[:, a]), (WH[:, piece, sl], WL[:, piece, sl]),
                                     start=(k == 0), stop=(k == FT - 1))
                    last.then_inc(act_used, 1)

            expert(0, 0, first=True)
            with pe.Fori(0, (NE - 2) // 2) as pair:
                for s in range(2):
                    expert(pair * 2 + (s + 1), 1 - s)
            expert(NE - 1, 1, last_one=True)


def kernel(**inputs):
    import numpy as np
    import concourse.bacc as bacc
    from concourse import mybir
    from concourse.bass_utils import run_bass_kernel_spmd as run

    A = {k: np.asarray(v) for k, v in inputs.items()}
    P, E = 128, 16

    def gate_up(g, u):
        w = np.stack([g, u], axis=-3)
        lead = w.shape[:-3]
        w = w.reshape(*lead, 2, -1, P, 2, P)
        n = len(lead)
        w = w.transpose(*range(n), n + 4, n + 1, n, n + 3, n + 2)
        return np.ascontiguousarray(w.reshape(*lead, P, -1))

    def down(w):
        lead = w.shape[:-2]
        n = len(lead)
        w = w.reshape(*lead, 256, -1, P).transpose(*range(n), n + 2, n + 1, n)
        return np.ascontiguousarray(w.reshape(*lead, P, -1))

    halves = lambda v: v.reshape(2, P).T
    arrays = {
        "x": A["x"],
        "ctx": np.ascontiguousarray(A["ctx_1024"].transpose(2, 0, 1).reshape(2, P, 8, 256).transpose(1, 2, 0, 3)),
        "wu": np.ascontiguousarray(np.concatenate([halves(A["L0_xattn_w"].reshape(-1)), halves(A["L0_xattn_u"].reshape(-1))], axis=1)),
        "g": np.ascontiguousarray(np.broadcast_to(np.concatenate([A["g_xattn"], A["g_ffn"]]), (P, 2))),
        "gatew": np.ascontiguousarray(A["L0_ffn_gate_w"].reshape(E, 2, P).transpose(2, 1, 0)),
        "shgu": gate_up(A["L0_ffn_sh_gate_w"], A["L0_ffn_sh_up_w"]),
        "shd": down(A["L0_ffn_sh_down_w"]),
        "gu": gate_up(A["L0_ffn_gw"], A["L0_ffn_up_w"]),
        "dn": down(A["L0_ffn_down_w"]),
        "fb": np.ascontiguousarray(np.concatenate([A["L0_ffn_gb"].reshape(E, 8, P).transpose(0, 2, 1),
                                                   A["L0_ffn_up_b"].reshape(E, 8, P).transpose(0, 2, 1)], axis=2)),
        "db": A["L0_ffn_down_b"],
    }
    nc = bacc.Bacc("TRN2", target_bir_lowering=False, num_devices=1)
    aps = [nc.dram_tensor(f"in_{k}", a.shape, mybir.dt.from_np(a.dtype), kind="ExternalInput").ap() for k, a in arrays.items()]
    out = nc.dram_tensor("out_0", (8, 256, 256), mybir.dt.float32, kind="ExternalOutput").ap()
    flamingo_layer(nc, *aps, out)
    r = run(nc, [{f"in_{k}": a for k, a in arrays.items()}], core_ids=[0])
    return r.results[0]["out_0"]
```

```python
import concourse.bass as bass
from concourse import mybir
from contextlib import ExitStack


def flamingo_layer(nc, x_in, ctx_in, wu_in, g_in, gatew_in, shgu_in, shd_in, gu_in, dn_in, fb_in, db_in, out):
    f32, f32r, bf16, fp16 = mybir.dt.float32, mybir.dt.float32r, mybir.dt.bfloat16, mybir.dt.float16
    i32, u32 = mybir.dt.int32, mybir.dt.uint32
    ALU, ACT, AX = mybir.AluOpType, mybir.ActivationFunctionType, mybir.AxisListType

    P = 128
    B, T, C = 8, 256, 256
    H = C // P
    NT = B * T // P
    NE, F, SH = 16, 1024, 512
    CAP = B * T // NE * 2
    SEG = T + 1
    L = H * SEG + 1
    ROW = C + NE
    FT = F // P
    ST = SH // P
    PC = 512
    GUP, DNP = FT, FT * C // PC
    NP = GUP + DNP
    CT = 512
    NCH = B * T // CT
    TPC = CT // P
    ROUNDS = 16
    RPC = 6
    EPS = 1e-5
    TOP = 16.635532
    BOTTOM = -89.0
    LO0, W0 = -96.0, 32.0

    rows = nc.dram_tensor("h_rows", (B * T, ROW), f32, kind="Internal").ap()
    out_rows = out.rearrange("b t d -> (b t) d")

    with ExitStack() as ctx:
        def sb(name, shape, dt=f32):
            return ctx.enter_context(nc.sbuf_tensor(name, shape, dt))

        def sem(name):
            return ctx.enter_context(nc.semaphore(name))

        X = sb("X", [P, NT, C])
        WH = sb("WH", [P, NP, PC], f32r)
        WL = sb("WL", [P, NP, PC], f32r)
        RAWA = sb("RAWA", [P, 4 * PC])
        RAWB = sb("RAWB", [P, 4 * PC])
        RAWD = sb("RAWD", [P, 4 * PC])
        AH = sb("AH", [P, FT * CAP], f32r)
        AL = sb("AL", [P, FT * CAP], f32r)
        HTH = sb("HTH", [P, H, B * T], f32r)
        HTL = sb("HTL", [P, H, B * T], f32r)
        XTH = sb("XTH", [P, H, CAP], f32r)
        XTL = sb("XTL", [P, H, CAP], f32r)
        GSTRIP = P - NE
        GWH = sb("GWH", [P, H, GSTRIP + P], f32r)
        GWL = sb("GWL", [P, H, GSTRIP + P], f32r)
        GW = sb("GW", [P, H, GSTRIP + P])
        ident = sb("ident", [P, P])
        identg = sb("identg", [P, P])
        diag = sb("diag", [P, H, P])
        diagg = sb("diagg", [P, H, P])
        WU = sb("WU", [P, 2 * H])
        EWU = sb("EWU", [P, 2 * H])
        GIN = sb("GIN", [P, 2])
        TG = sb("TG", [P, 2])
        eps = sb("eps", [P, 1])
        D = sb("D", [P, L])
        KB = [sb(f"KB{s}", [P, H, T]) for s in range(4)]
        HB = [sb(f"HB{s}", [P, 2, C]) for s in range(2)]
        MV1 = sb("MV1", [P, NT, 2])
        NR1 = sb("NR1", [P, NT])
        BI1 = sb("BI1", [P, NT])
        R1 = sb("R1", [P, NT])
        MV2 = sb("MV2", [P, NT, 2])
        BS = sb("BS", [P, 2 * NT, 6])
        R2 = sb("R2", [P, NT])
        T2 = sb("T2", [P, NT])
        NB2 = sb("NB2", [P, NT])
        same = sb("same", [P, P], bf16)
        before = sb("before", [P, P], bf16)
        own_block = sb("own_block", [P, P])
        spread = sb("spread", [P, P], fp16)
        bitmat, rowmat = (KB[n][:, 0, 0:P].bitcast(i32) for n in range(2))
        masked, earlier = (KB[n][:, 1, 0:P] for n in range(2))
        TIDS = KB[2][:, 0, 0:P].bitcast(fp16)
        colnum = sb("colnum", [P, 1], i32)
        colf = sb("colf", [P, 1])
        iota3 = sb("iota3", [P, 3])
        pick = sb("pick", [P, 2, 8])
        IDXALL = sb("IDXALL", [P, NE, 2], u32)
        IDX = [sb(f"IDX{s}", [P, 2], u32) for s in range(2)]
        SIX = [sb(f"SIX{s}", [P, 2], u32) for s in range(2)]
        SCC = [sb(f"SCC{s}", [P, 2]) for s in range(2)]
        FB = [sb(f"FB{s}", [P, 2 * FT]) for s in range(2)]
        small = sb("small", [P, 16])
        mids = sb("mids", [P, 3])
        geq = sb("geq", [P, 3])
        cntb = sb("cntb", [P, 4], bf16)

        ARENA = 2 * 6 * L + 8 * 512
        AR = sb("AR", [P, ARENA])
        top = [0]

        def view(n, at=None):
            a = top[0] if at is None else at
            if at is None:
                top[0] += n
            assert a + n <= ARENA
            return AR[:, a:a + n]
        EK, KV, SA, RA, SB_, RB = [[view(L) for _ in range(2)] for _ in range(6)]
        E_, Q, RQ, TT = [[view(512) for _ in range(2)] for _ in range(4)]
        top[0] = 0
        SG = [view(512) for _ in range(2)]
        AF = [view(512) for _ in range(2)]
        KEY, MHI, MGE, PHI, PGE, SCO, TMPA, TMPB = [view(T) for _ in range(8)]
        SLT = view(NT * NE)
        SHIF, SLOF = [view(NT * NE // 2).bitcast(fp16) for _ in range(2)]
        SINT = view(NT * NE)
        SINT2 = view(NT * NE)
        SC = view(NT * NE)
        IDH = view(NE * 8).bitcast(fp16)
        IDM = PGE
        IDR = view(NE * 2)
        SY = [view(C) for _ in range(2)]
        rest = top[0]
        OA = view(NT * NE * 8).bitcast(fp16)
        OB = view(NT * NE * 8).bitcast(fp16)
        top[0] = rest
        G = [view(2 * ROW) for _ in range(2)]
        Y = [view(2 * C) for _ in range(2)]
        DB = [view(C) for _ in range(2)]

        PS = [ctx.enter_context(nc.psum_tensor(f"PS{i}", [P, 512], f32)) for i in range(8)]
        NUM, DEN, TR, LG = PS[0:2], PS[2:4], PS[4:6], PS[6]
        OUT = PS[4:6]
        CNT = PS[7]

        wu_arrived, gates_arrived = sem("wu_arrived"), sem("gates_arrived")
        ctx_arrived = [sem(f"ctx_arrived{b}") for b in range(B)]
        x_arrived = [sem(f"x_arrived{b}") for b in range(B)]
        gw_arrived = sem("gw_arrived")
        rawa_arrived, rawb_arrived, rawd_arrived = sem("rawa_arrived"), sem("rawb_arrived"), sem("rawd_arrived")
        fb_arrived = [sem(f"fb_arrived{s}") for s in range(2)]
        db_arrived = [sem(f"db_arrived{s}") for s in range(2)]
        h_stored = [sem(f"h_stored{s}") for s in range(2)]
        scores_stored = sem("scores_stored")
        out_stored = sem("out_stored")
        pool_consts, routing_consts = sem("pool_consts"), sem("routing_consts")
        decay_exp, gates_tanh = sem("decay_exp"), sem("gates_tanh")
        dve_consts, den_consts, num_consts = sem("dve_consts"), sem("den_consts"), sem("num_consts")
        ln1_stats, ln1_rstd, ln1_affine = sem("ln1_stats"), sem("ln1_rstd"), sem("ln1_affine")
        act_order, dve_order, pool_order = sem("act_order"), sem("dve_order"), sem("pool_order")
        ek_ready, kv_ready, scans_done = sem("ek_ready"), sem("kv_ready"), sem("scans_done")
        den_done, num_done = sem("den_done"), sem("num_done")
        e_ready, q_ready, rq_ready, t_ready, x1_ready = sem("e_ready"), sem("q_ready"), sem("rq_ready"), sem("t_ready"), sem("x1_ready")
        ln2_stats, ln2_rstd, ln2_affine = sem("ln2_stats"), sem("ln2_rstd"), sem("ln2_affine")
        h_ready, ht_ready, hthi_ready, htlo_ready = sem("h_ready"), sem("ht_ready"), sem("hthi_ready"), sem("htlo_ready")
        logits_done = sem("logits_done")
        w_hi, w0_lo, w_lo, wd_lo = sem("w_hi"), sem("w0_lo"), sem("w_lo"), sem("wd_lo")
        key_ready, scores_ready, scores_turned, scores_laid = sem("key_ready"), sem("scores_ready"), sem("scores_turned"), sem("scores_laid")
        counted, totals = sem("counted"), sem("totals")
        step_order = sem("step_order")
        gu_done, silu_done, gu_free = sem("gu_done"), sem("silu_done"), sem("gu_free")
        acthi_done, actlo_done, act_used = sem("acthi_done"), sem("actlo_done"), sem("act_used")
        down_read, shared_added = sem("down_read"), sem("shared_added")
        slots_turned, slots_ready, onehots, ids_done, idx_ready = sem("slots_turned"), sem("slots_ready"), sem("onehots"), sem("ids_done"), sem("idx_ready")
        ids_masked, ids_spread = sem("ids_masked"), sem("ids_spread")
        tails, tail_tot = sem("tails"), sem("tail_tot")
        rows_gathered = [sem(f"rows_gathered{s}") for s in range(2)]
        xt_turned, xthi_done, xtlo_done = sem("xt_turned"), sem("xthi_done"), sem("xtlo_done")
        y_biased, y_ready, scattered = sem("y_biased"), sem("y_ready"), sem("scattered")
        idx_copied = sem("idx_copied")
        kept, rows_known = sem("kept"), sem("rows_known")

        NPC = 4
        ctx_v = ctx_in
        block = ctx.enter_context(nc.Block())

        SN = NCH * ST
        SPIECES = ST + ST * C // PC
        SBASE = GUP - 2

        def pick_expert(ap, e):
            if isinstance(e, int):
                return ap[e]
            return ap[bass.ds(e, 1), :, :].rearrange("o p n -> (o p) n")

        def raw_of(piece):
            return (RAWA, RAWB, RAWD)[piece // 4][:, piece % 4 * PC:(piece % 4 + 1) * PC]

        def raw_shared(piece):
            return RAWA[:, piece * PC:(piece + 1) * PC] if piece < ST else RAWB[:, (piece - ST) * PC:(piece - ST + 1) * PC]

        def tokens(t):
            return t[:, 1:1 + H * SEG].rearrange("p (h t) -> p h t", h=H)[:, :, 0:T]

        @block.sync
        def _(sp):
            sp.dma_start(WU[:], wu_in).then_inc(wu_arrived, 16)

            def load_batch(b):
                if b >= 4:
                    sp.wait_ge(kv_ready, b - 3)
                sp.dma_start(KB[b % 4][:], ctx_in[:, b, :, :]).then_inc(ctx_arrived[b], 16)
                sp.dma_start(X[:, 2 * b:2 * b + 2, :], x_in[b].rearrange("(i p) d -> p i d", p=P)).then_inc(x_arrived[b], 16)
            load_batch(0)
            sp.dma_start(GIN[:], g_in).then_inc(gates_arrived, 16)
            for b in range(1, 4):
                load_batch(b)
            sp.dma_start(RAWA[:], shgu_in).then_inc(rawa_arrived, 16)
            sp.dma_start(RAWB[:, 0:ST * C], shd_in).then_inc(rawb_arrived, 16)
            sp.wait_ge(dve_consts, 1)
            sp.dma_start(GW[:, :, GSTRIP:GSTRIP + NE], gatew_in).then_inc(gw_arrived, 16)
            for b in range(4, B):
                load_batch(b)
            sp.dma_start(RAWD[:], dn_in[0]).then_inc(rawd_arrived, 16)
            for b in range(B):
                sp.wait_ge(h_ready, 2 * (b + 1))
                sp.dma_start(rows[b * T:(b + 1) * T, 0:C].rearrange("(i p) d -> p i d", p=P), HB[b % 2][:]).then_inc(h_stored[b % 2], 16)
            sp.wait_ge(w0_lo, ST)
            sp.dma_start(RAWA[:], gu_in[0, :, 0:4 * PC]).then_inc(rawa_arrived, 16)
            sp.wait_ge(w0_lo, SPIECES)
            sp.dma_start(RAWB[:], gu_in[0, :, 4 * PC:8 * PC]).then_inc(rawb_arrived, 16)
            sp.dma_start(FB[0][:], fb_in[0]).then_inc(fb_arrived[0], 16)
            out_chunks = out_rows.rearrange("(c i p) d -> c p i d", p=P, i=TPC)

            def store_shared(c):
                sp.wait_ge(shared_added, TPC * c + (TPC + 2))
                dst = out_chunks[c] if isinstance(c, int) else out_chunks[bass.ds(c, 1), :, :, :].rearrange("o p i d -> (o p) i d")
                sp.dma_start(dst, X[:, bass.ds(c * TPC, TPC), :]).then_inc(out_stored, 16)

            with sp.Fori(0, NCH - 2) as c:
                store_shared(c)
            sp.wait_ge(scores_laid, 2)
            sp.dma_start(rows[:, C:ROW].rearrange("(i p) e -> p i e", p=P), SC.rearrange("p (i e) -> p i e", e=NE)).then_inc(scores_stored, 16)
            for c in range(NCH - 2, NCH):
                store_shared(c)
            sp.wait_ge(idx_ready, 1)
            sp.dma_start(DB[0][:], db_in[0:1, :].rearrange("o d -> (o d)").partition_broadcast(P)).then_inc(db_arrived[0], 16)

            def load_expert(e, s, first=False):
                if isinstance(e, int) and e == 1:
                    sp.wait_ge(w0_lo, SPIECES + 4)
                else:
                    sp.wait_ge(w_lo, GUP * (e - 2) + (GUP - SBASE + 4))
                sp.dma_start(RAWA[:], pick_expert(gu_in, e)[:, 0:4 * PC]).then_inc(rawa_arrived, 16)
                if isinstance(e, int) and e == 1:
                    sp.wait_ge(w0_lo, SPIECES + SBASE)
                    sp.wait_ge(w_lo, GUP - SBASE)
                else:
                    sp.wait_ge(w_lo, GUP * (e - 2) + (GUP - SBASE + 8))
                sp.dma_start(RAWB[:], pick_expert(gu_in, e)[:, 4 * PC:8 * PC]).then_inc(rawb_arrived, 16)
                sp.wait_ge(wd_lo, DNP * e)
                sp.dma_start(RAWD[:], pick_expert(dn_in, e)).then_inc(rawd_arrived, 16)
                if not first:
                    sp.wait_ge(y_biased, 2 * (e - 1))
                sp.dma_start(FB[s][:], pick_expert(fb_in, e)).then_inc(fb_arrived[s], 16)
                sp.dma_start(DB[s][:], (db_in[e:e + 1, :] if isinstance(e, int) else db_in[bass.ds(e, 1), :])
                             .rearrange("o d -> (o d)").partition_broadcast(P)).then_inc(db_arrived[s], 16)

            load_expert(1, 1, first=True)
            with sp.Fori(0, (NE - 2) // 2) as pair:
                for s in range(2):
                    load_expert(pair * 2 + (s + 2), s)
            sp.wait_ge(out_stored, 16 * NCH)
            sp.wait_ge(scattered, 32 * NE)
            sp.wait_ge(scores_stored, 16)
            for s in range(2):
                sp.wait_ge(h_stored[s], 16 * B // 2)

        @block.gpsimd
        def _(pool):
            nc.gpsimd.memset(ident[:], 0.0).then_inc(pool_order, 1)
            pool.wait_ge(pool_order, 1)
            nc.gpsimd.affine_select(out=ident[:], in_=ident[:], compare_op=ALU.not_equal, fill=1.0, base=0,
                                    pattern=[[-1, P]], channel_multiplier=1).then_inc(pool_consts, 1)
            n = [1]

            def mark(ins):
                n[0] += 1
                ins.then_inc(pool_order, 1)

            nc.gpsimd.iota(iota3[:], pattern=[[1, 3]], base=1, channel_multiplier=0,
                           allow_small_or_imprecise_dtypes=True).then_inc(pool_consts, 1)
            nc.gpsimd.iota(small[:, 8:16].bitcast(i32), pattern=[[1, 8]], base=P, channel_multiplier=-1).then_inc(pool_consts, 1)
            nc.gpsimd.iota(colnum[:], pattern=[[0, 1]], base=0, channel_multiplier=1).then_inc(pool_consts, 1)
            for s in range(2):
                for t in (EK[s], KV[s]):
                    mark(nc.gpsimd.memset(t[:, 0:L:SEG], 0.0))
            pads = n[0]

            def product(b):
                pool.wait_ge(pool_order, pads)
                if b >= 2:
                    pool.wait_ge(num_done, b - 1)
                pool.wait_ge(ek_ready, b + 1)
                nc.gpsimd.tensor_tensor(tokens(KV[b % 2]), tokens(EK[b % 2]), KB[b % 4][:], ALU.mult).then_inc(kv_ready, 1)

            def shared_weight_lo(q):
                pool.wait_ge(w_hi, q + 1)
                nc.gpsimd.tensor_tensor(WL[:, SBASE + q, :], raw_shared(q), WH[:, SBASE + q, :].bitcast(f32),
                                        ALU.subtract).then_inc(w0_lo, 1)

            product(0)
            for i in range(B + 3):
                b = i - 2
                if 0 <= b < B:
                    pool.wait_ge(t_ready, b + 1)
                    pool.wait_ge(x_arrived[b], 16)
                    nc.gpsimd.tensor_tensor(X[:, 2 * b:2 * b + 2, :], X[:, 2 * b:2 * b + 2, :],
                                            TT[b % 2].rearrange("p (i c) -> p i c", i=2), ALU.add).then_inc(x1_ready, 1)
                if i + 1 < B:
                    product(i + 1)
                if 1 <= i <= SPIECES:
                    shared_weight_lo(i - 1)
                if i == B - 1:
                    nc.gpsimd.iota(bitmat, pattern=[[-1, P]], base=256, channel_multiplier=1).then_inc(routing_consts, 1)
                    nc.gpsimd.iota(rowmat, pattern=[[1, P]], base=0, channel_multiplier=0).then_inc(routing_consts, 1)
                    nc.gpsimd.iota(TIDS, pattern=[[P, NT], [0, NE]], base=0, channel_multiplier=1,
                                   allow_small_or_imprecise_dtypes=True).then_inc(routing_consts, 1)

            def wait_all(*waits):
                counts = [v if isinstance(v, int) else pool.to_reg(v) for _, v in waits]
                pool.wait_ge(pool_consts, NPC)
                for (signal, _), count in zip(waits, counts):
                    pool.wait_ge(signal, count)

            def act_lo(c, ft):
                sl = slice(ft * CT, (ft + 1) * CT)
                wait_all((acthi_done, c * ST + (ft + 1)))
                nc.gpsimd.tensor_tensor(AL[:, sl], AF[ft % 2], AH[:, sl].bitcast(f32), ALU.subtract).then_inc(actlo_done, 1)

            def add_shared(c):
                for tt in range(TPC):
                    wait_all((down_read, TPC + c * TPC + (tt + 1)))
                    xs = X[:, c * TPC + tt, :] if isinstance(c, int) else X[:, bass.ds(c * TPC + tt, 1), :].rearrange("p o d -> p (o d)")
                    nc.gpsimd.tensor_tensor(xs, xs, SY[tt % 2], ALU.add).then_inc(shared_added, 1)

            def first_lo(q):
                pool.wait_ge(w_hi, SPIECES + q + 1)
                nc.gpsimd.tensor_tensor(WL[:, q, :], raw_of(q), WH[:, q, :].bitcast(f32), ALU.subtract).then_inc(w0_lo, 1)

            with pool.Fori(0, NCH - 2) as c:
                for ft in range(ST):
                    act_lo(c, ft)
                add_shared(c)

            def fetch(e, s):
                nc.gpsimd.tensor_copy(IDX[s][:], index_of(e)).then_inc(idx_copied, 1)
                wait_all((idx_copied, e + 1))
                for j in range(2):
                    pool.indirect_dma_start(G[s][:, j * ROW:(j + 1) * ROW], None, rows,
                                            bass.IndirectOffsetOnAxis(ap=IDX[s][:, j:j + 1], axis=0)).then_inc(rows_gathered[s], 16)

            def index_of(e):
                return IDXALL[:, e, :] if isinstance(e, int) else IDXALL[:, bass.ds(e, 1), :].rearrange("p o j -> p (o j)")

            def keep_scores(e, s):
                sc = G[s][:, C + e:C + e + ROW + 1:ROW] if isinstance(e, int) else G[s][:, bass.ds(e + C, 2, step=ROW)]
                wait_all((rows_gathered[s], 16 * (e - s) + 32))
                nc.gpsimd.tensor_copy(SCC[s][:], sc).then_inc(kept, 1)

            def finish(e, s):
                before_it = (out_stored, 16 * NCH) if isinstance(e, int) and e == 0 else (scattered, 32 * e)
                wait_all(before_it)
                nc.gpsimd.tensor_copy(SIX[s][:], index_of(e)).then_inc(rows_known, 1)
                for j in range(2):
                    wait_all((kept, e + 1), (y_biased, 2 * e + (j + 1)))
                    nc.gpsimd.tensor_scalar(Y[s][:, j * C:(j + 1) * C], Y[s][:, j * C:(j + 1) * C],
                                            SCC[s][:, j:j + 1], TG[:, 1:2], ALU.mult, ALU.mult).then_inc(y_ready, 1)
                wait_all((y_ready, 2 * e + 2), (rows_known, e + 1))
                for j in range(2):
                    pool.indirect_dma_start(out_rows, bass.IndirectOffsetOnAxis(ap=SIX[s][:, j:j + 1], axis=0),
                                            Y[s][:, j * C:(j + 1) * C], None, compute_op=ALU.add).then_inc(scattered, 16)

            for ft in range(ST):
                act_lo(NCH - 2, ft)
                first_lo(ft)
            add_shared(NCH - 2)
            for ft in range(ST):
                act_lo(NCH - 1, ft)
                if ft < SBASE - ST:
                    first_lo(ST + ft)
            pool.wait_ge(idx_ready, 1)
            pool.wait_ge(scores_stored, 16)
            for s in range(2):
                pool.wait_ge(h_stored[s], 16 * B // 2)
            fetch(0, 0)
            add_shared(NCH - 1)

            def down_lo(e, q):
                wait_all((w_hi, SPIECES + NP * e + (GUP + q + 1)))
                nc.gpsimd.tensor_tensor(WL[:, GUP + q, :], RAWD[:, q * PC:(q + 1) * PC],
                                        WH[:, GUP + q, :].bitcast(f32), ALU.subtract).then_inc(wd_lo, 1)

            def expert(e, s, first=False, last=False):
                keep_scores(e, s)
                if not last:
                    fetch(e + 1, 1 - s)
                if not first:
                    finish(e - 1, 1 - s)
                if not last:
                    for q in range(DNP):
                        down_lo(e + 1, q)

            for q in range(DNP):
                down_lo(0, q)
            expert(0, 0, first=True)
            with pool.Fori(0, (NE - 2) // 2) as pair:
                for s in range(2):
                    expert(pair * 2 + (s + 1), 1 - s)
            expert(NE - 1, 1, last=True)
            finish(NE - 1, 1)

        @block.scalar
        def _(act):
            n = [0]

            def link(ins):
                n[0] += 1
                ins.then_inc(act_order, 1)
                act.wait_ge(act_order, n[0])

            nc.scalar.preload_act_table_set("natural_log_exp_and_others")
            act.wait_ge(wu_arrived, 16)
            nc.scalar.activation(EWU[:], WU[:], ACT.Exp).then_inc(decay_exp, 1)

            def exp_k(b):
                act.wait_ge(ctx_arrived[b], 16)
                if b >= 2:
                    act.wait_ge(den_done, b - 1)
                    act.wait_ge(kv_ready, b - 1)
                else:
                    act.wait_ge(pool_order, 5)
                nc.scalar.activation(tokens(EK[b % 2]), KB[b % 4][:], ACT.Exp).then_inc(ek_ready, 1)

            def ln1(g):
                act.wait_ge(ln1_stats, g + 1)
                a = slice(4 * g, 4 * g + 4)
                link(nc.scalar.activation(R1[:, a], MV1[:, a, 1], ACT.Ln, bias=eps[:, 0:1]))
                nc.scalar.activation(R1[:, a], R1[:, a], ACT.Exp, scale=-0.5).then_inc(ln1_rstd, 1)

            def hi_weight(piece, raw):
                nc.scalar.activation(WH[:, piece, :], raw, ACT.Copy).then_inc(w_hi, 1)

            exp_k(0)
            exp_k(1)
            act.wait_ge(gates_arrived, 16)
            nc.scalar.activation(TG[:], GIN[:], ACT.Tanh).then_inc(gates_tanh, 1)
            nc.scalar.preload_act_table_set("natural_log_exp_and_others")
            for i in range(B + 3):
                b = i - 3
                if 0 <= b < B:
                    act.wait_ge(ln2_affine, b + 1)
                    if b >= 2:
                        act.wait_ge(ht_ready, b - 1)
                        act.wait_ge(h_stored[b % 2], 16 * (b // 2))
                    for j in range(2):
                        t = 2 * b + j
                        nc.scalar.activation(HB[b % 2][:, j, :], X[:, t, :], ACT.Identity, scale=R2[:, t:t + 1],
                                             bias=NB2[:, t:t + 1]).then_inc(h_ready, 1)
                if 2 <= i + 1 < B:
                    exp_k(i + 1)
                if i == 0:
                    act.wait_ge(dve_consts, 1)
                    ln1(0)
                b = i - 3
                if 0 <= b < B:
                    act.wait_ge(ht_ready, b + 1)
                    nc.scalar.activation(HTH[:, :, b * T:(b + 1) * T], TR[b % 2][:].rearrange("p (k t) -> p k t", k=H),
                                         ACT.Copy).then_inc(hthi_ready, 1)
                b = i
                if b < B:
                    act.wait_ge(ln1_affine, 1 + b // 2)
                    if b >= 2:
                        act.wait_ge(q_ready, b - 1)
                    for j in range(2):
                        t = 2 * b + j
                        nc.scalar.activation(E_[b % 2][:, j * C:(j + 1) * C], X[:, t, :], ACT.Exp, scale=NR1[:, t:t + 1],
                                             bias=BI1[:, t:t + 1]).then_inc(e_ready, 1)
                b = i - 1
                if 0 <= b < B:
                    act.wait_ge(q_ready, b + 1)
                    link(nc.scalar.activation(Q[b % 2], Q[b % 2], ACT.Ln))
                    if b >= 2:
                        act.wait_ge(t_ready, b - 1)
                    nc.scalar.activation(RQ[b % 2], Q[b % 2], ACT.Exp, scale=-1.0).then_inc(rq_ready, 1)
                b = i - 2
                if 0 <= b < B:
                    act.wait_ge(ln2_stats, b + 1)
                    a = slice(2 * b, 2 * b + 2)
                    link(nc.scalar.activation(R2[:, a], MV2[:, a, 1], ACT.Ln, bias=eps[:, 0:1]))
                    nc.scalar.activation(R2[:, a], R2[:, a], ACT.Exp, scale=-0.5).then_inc(ln2_rstd, 1)
                if i % 2 == 1 and i + 1 < B:
                    ln1((i + 1) // 2)
                if 1 <= i <= SPIECES:
                    act.wait_ge(rawa_arrived if i <= ST else rawb_arrived, 16)
                    hi_weight(SBASE + i - 1, raw_shared(i - 1))

            act.wait_ge(key_ready, 1)
            nc.scalar.activation(SCO, LG[:, 0:T], ACT.Sigmoid).then_inc(scores_ready, 1)

            def first_hi(q):
                if q % 4 == 0:
                    act.wait_ge((rawa_arrived, rawb_arrived, rawd_arrived)[q // 4], (32, 32, 16)[q // 4])
                if q >= SBASE + ST:
                    act.wait_ge(act_used, SN + 2 * (q - SBASE - ST + 1))
                elif q >= SBASE:
                    act.wait_ge(gu_done, SN - ST + (q - SBASE + 1))
                hi_weight(q, raw_of(q))

            def act_silu(c, ft):
                act.wait_ge(gu_done, c * ST + (ft + 1))
                act.wait_ge(gu_free, c * ST + (ft + 1))
                nc.scalar.activation(SG[ft % 2], PS[ft % 2][:], ACT.Silu).then_inc(silu_done, 1)

            def chunk(c, expert0=(), scores=False, last=False):
                pieces = list(expert0)

                def act_hi(ft):
                    act.wait_ge(gu_free, c * ST + (ft + 3))
                    act.wait_ge(act_used, c * ST + (ft + 1))
                    nc.scalar.activation(AH[:, ft * CT:(ft + 1) * CT], AF[ft % 2], ACT.Copy).then_inc(acthi_done, 1)
                if scores:
                    for j in range(2):
                        act.wait_ge(scores_turned, 2)
                        nc.scalar.activation(SC.rearrange("p (b j e) -> p b j e", j=2, e=NE)[:, :, j, :],
                                             PS[6][:, j * P:(j + 1) * P].rearrange("p (b e) -> p b e", e=NE), ACT.Copy).then_inc(scores_laid, 1)
                for ft in range(1, ST):
                    act_silu(c, ft)
                    act_hi(ft - 1)
                    if pieces:
                        first_hi(pieces.pop(0))
                act_hi(ST - 1)
                for q in pieces:
                    first_hi(q)
                if not last:
                    act_silu(c + 1, 0)
                act.wait_ge(act_used, ST + c * ST + ST)
                for tt in range(TPC):
                    act.wait_ge(shared_added, TPC * c + (tt + 1))
                    nc.scalar.activation(SY[tt % 2], OUT[tt // 2][:, tt % 2 * C:(tt % 2 + 1) * C], ACT.Copy,
                                         scale=TG[:, 1:2]).then_inc(down_read, 1)

            act_silu(0, 0)
            with act.Fori(0, NCH - 2) as c:
                chunk(c)
            chunk(NCH - 2, range(0, ST), scores=True)
            chunk(NCH - 1, range(ST, GUP), last=True)

            def xt_hi(e):
                act.wait_ge(xt_turned, e + 1)
                nc.scalar.activation(XTH[:], PS[6][:].rearrange("p (k t) -> p k t", k=H), ACT.Copy).then_inc(xthi_done, 1)

            xt_hi(0)
            for q in range(GUP, NP):
                first_hi(q)

            def expert(e, s, last=False):
                act.wait_ge(fb_arrived[s], 8 * (e - s) + 16)
                for f in range(FT):
                    act.wait_ge(gu_done, SN + FT * e + (f + 1))
                    act.wait_ge(gu_free, SN + FT * e + (f + 1))
                    nc.scalar.activation(SG[f % 2][:, 0:CAP], PS[f % 4][:, 0:CAP], ACT.Silu, bias=FB[s][:, f:f + 1]).then_inc(silu_done, 1)
                    if f >= 1:
                        hi_of(e, f - 1)
                        if not last:
                            next_hi(e, f - 1)
                hi_of(e, FT - 1)
                if last:
                    return
                next_hi(e, GUP - 1)
                next_hi(e, GUP)
                xt_hi(e + 1)
                for q in range(GUP + 1, NP):
                    next_hi(e, q)

            def hi_of(e, f):
                act.wait_ge(gu_free, SN + FT * e + (f + 3))
                act.wait_ge(act_used, SN + FT * e + (f + 1 - FT + ST))
                nc.scalar.activation(AH[:, f * CAP:(f + 1) * CAP], AF[f % 2][:, 0:CAP], ACT.Copy).then_inc(acthi_done, 1)

            def next_hi(e, q):
                if q % 4 == 0:
                    if q < GUP:
                        act.wait_ge((rawa_arrived, rawb_arrived)[q // 4], 16 * e + 48)
                    else:
                        act.wait_ge(rawd_arrived, 16 * e + 32)
                if q < GUP:
                    act.wait_ge(gu_done, SN + FT * e + (q + 1))
                else:
                    act.wait_ge(act_used, ST + SN + FT * e + 2 * (q - GUP + 1))
                hi_weight(q, raw_of(q))

            expert(0, 0)
            with act.Fori(0, (NE - 2) // 2) as pair:
                for s in range(2):
                    expert(pair * 2 + (s + 1), 1 - s)
            expert(NE - 1, 1, last=True)

        @block.vector
        def _(dve):
            n = [0]

            def mark(ins):
                n[0] += 1
                ins.then_inc(dve_order, 1)

            def link(ins):
                mark(ins)
                dve.wait_ge(dve_order, n[0])

            V = nc.vector
            mark(V.memset(D[:], 1.0))
            mark(V.memset(eps[:], EPS))
            link(V.memset(GW[:], 0.0))
            V.memset(small[:, 0:1], LO0).then_inc(dve_consts, 1)
            dve.wait_ge(dve_consts, 1)
            dve.wait_ge(decay_exp, 1)
            for h in range(H):
                mark(V.tensor_scalar(D[:, h * SEG + 1:(h + 1) * SEG], D[:, h * SEG + 1:(h + 1) * SEG], EWU[:, h:h + 1], None, ALU.mult))
            link(V.memset(D[:, 0:L:SEG], 0.0))

            def ln1(g):
                for t in range(4 * g, 4 * g + 4):
                    dve.wait_ge(x_arrived[t // 2], 16)
                    mark(V.bn_stats(BS[:, t, :], X[:, t, :]))
                dve.wait_ge(dve_order, n[0])
                for t in range(4 * g, 4 * g + 4):
                    ins = V.bn_aggr(MV1[:, t, :], BS[:, t, :])
                    if t < 4 * g + 3:
                        mark(ins)
                    else:
                        ins.then_inc(ln1_stats, 1)

            def ln1_scale(g):
                a = slice(4 * g, 4 * g + 4)
                dve.wait_ge(ln1_rstd, g + 1)
                mark(V.tensor_scalar(NR1[:, a], R1[:, a], -1.0, None, ALU.mult))
                V.tensor_tensor(BI1[:, a], MV1[:, a, 0], R1[:, a], ALU.mult).then_inc(ln1_affine, 1)

            dve.wait_ge(pool_consts, NPC)
            for h in range(H):
                ins = V.tensor_scalar(diag[:, h, :], ident[:], EWU[:, H + h:H + h + 1], None, ALU.mult)
                ins.then_inc(den_consts, 1)

            def num_matrices():
                dve.wait_ge(gates_tanh, 1)
                V.tensor_scalar(identg[:], ident[:], TG[:, 0:1], None, ALU.mult).then_inc(num_consts, 1)
                dve.wait_ge(den_consts, H)
                for h in range(H):
                    V.tensor_scalar(diagg[:, h, :], diag[:, h, :], TG[:, 0:1], None, ALU.mult).then_inc(num_consts, 1)

            def split_weight(count, piece, raw):
                dve.wait_ge(w_hi, count)
                V.tensor_tensor(WL[:, piece, :], raw, WH[:, piece, :].bitcast(f32), ALU.subtract).then_inc(w_lo, 1)

            lo, w, s_, four_w = (small[:, k:k + 1] for k in range(4))

            def routing_matrices():
                dve.wait_ge(routing_consts, 3)
                mi = masked.bitcast(i32)
                link(V.tensor_scalar(mi, bitmat, 15, None, ALU.bitwise_and))
                mark(V.tensor_scalar(same[:], mi, 0.0, None, ALU.is_equal))
                link(V.tensor_scalar(earlier, bitmat, 256.0, None, ALU.is_lt))
                mark(V.tensor_tensor(before[:], same[:], earlier, ALU.mult))
                link(V.tensor_scalar(bitmat, bitmat, 7, None, ALU.bitwise_and))
                mark(V.tensor_scalar(own_block[:], bitmat, 0.0, None, ALU.is_equal))
                link(V.tensor_scalar(small[:, 8:16].bitcast(i32), small[:, 8:16].bitcast(i32), 7, None, ALU.bitwise_and))
                for j in range(2):
                    mark(V.tensor_scalar(pick[:, j, :], small[:, 8:16].bitcast(i32), 0.0, None, ALU.is_equal))
                mark(V.tensor_scalar(rowmat, rowmat, 3, None, ALU.arith_shift_right))
                link(V.tensor_scalar(colnum[:], colnum[:], 3, None, ALU.arith_shift_right))
                link(V.tensor_copy(colf[:], colnum[:]))
                mark(V.tensor_scalar(spread[:], rowmat, colf[:, 0:1], None, ALU.is_equal))
                mark(V.memset(w, W0))
                link(V.tensor_scalar(mids[:], iota3[:], W0, LO0, ALU.mult, ALU.add))

            def newton(b):
                a = slice(2 * b, 2 * b + 2)
                dve.wait_ge(ln2_rstd, b + 1)
                link(V.tensor_tensor(T2[:, a], R2[:, a], R2[:, a], ALU.mult))
                link(V.scalar_tensor_tensor(T2[:, a], MV2[:, a, 1], EPS, T2[:, a], ALU.add, ALU.mult))
                link(V.tensor_scalar(T2[:, a], T2[:, a], -0.5, 1.5, ALU.mult, ALU.add))
                link(V.tensor_tensor(R2[:, a], R2[:, a], T2[:, a], ALU.mult))
                V.scalar_tensor_tensor(NB2[:, a], MV2[:, a, 0], -1.0, R2[:, a], ALU.mult, ALU.mult).then_inc(ln2_affine, 1)

            def attended(b):
                dve.wait_ge(rq_ready, b + 1)
                dve.wait_ge(num_done, b + 1)
                if b >= 2:
                    dve.wait_ge(x1_ready, b - 1)
                V.tensor_tensor(TT[b % 2], NUM[b % 2][:], RQ[b % 2], ALU.mult).then_inc(t_ready, 1)

            for i in range(B + 3):
                if 0 <= i - 2 < B and i >= B:
                    attended(i - 2)
                if 0 <= i - 3 < B:
                    newton(i - 3)
                if i % 2 == 0 and 0 < i < B:
                    ln1_scale(i // 2)
                if 0 <= i - 2 < B and i < B:
                    attended(i - 2)
                b = i
                if b < B:
                    s = b % 2
                    if i == 0:
                        dve.wait_ge(dve_order, n[0])
                    if b >= 2:
                        dve.wait_ge(den_done, b - 1)
                    dve.wait_ge(ek_ready, b + 1)
                    V.tensor_tensor_scan(SB_[s], D[:], EK[s], 0.0, ALU.mult, ALU.add).then_inc(scans_done, 1)
                    V.tensor_tensor_scan(RB[s][:, ::-1], D[:, ::-1], EK[s][:, ::-1], 0.0, ALU.mult, ALU.add).then_inc(scans_done, 1)
                    if b >= 2:
                        dve.wait_ge(num_done, b - 1)
                    dve.wait_ge(kv_ready, b + 1)
                    V.tensor_tensor_scan(SA[s], D[:], KV[s], 0.0, ALU.mult, ALU.add).then_inc(scans_done, 1)
                    V.tensor_tensor_scan(RA[s][:, ::-1], D[:, ::-1], KV[s][:, ::-1], 0.0, ALU.mult, ALU.add).then_inc(scans_done, 1)
                if i == 0:
                    ln1(0)
                    num_matrices()
                if i == 1:
                    ln1_scale(0)
                    ln1(1)
                b = i - 2
                if 0 <= b < B:
                    dve.wait_ge(x1_ready, b + 1)
                    for j in range(2):
                        mark(V.bn_stats(BS[:, NT + 2 * b + j, :], X[:, 2 * b + j, :]))
                    stats_at = n[0]
                b = i - 1
                if 0 <= b < B:
                    dve.wait_ge(den_done, b + 1)
                    dve.wait_ge(e_ready, 2 * b + 2)
                    if b >= 2:
                        dve.wait_ge(rq_ready, b - 1)
                    V.scalar_tensor_tensor(Q[b % 2], E_[b % 2], 1.0, DEN[b % 2][:], ALU.add, ALU.mult).then_inc(q_ready, 1)
                b = i - 2
                if 0 <= b < B:
                    dve.wait_ge(dve_order, stats_at)
                    mark(V.bn_aggr(MV2[:, 2 * b, :], BS[:, NT + 2 * b, :]))
                    V.bn_aggr(MV2[:, 2 * b + 1, :], BS[:, NT + 2 * b + 1, :]).then_inc(ln2_stats, 1)
                    if b == 0:
                        dve.wait_ge(gw_arrived, 16)
                        link(V.tensor_copy(GWH[:], GW[:]))
                        mark(V.tensor_tensor(GWL[:], GW[:], GWH[:].bitcast(f32), ALU.subtract))
                if i % 2 == 1 and 1 < i < B - 1:
                    ln1((i + 1) // 2)
                if i == B + 2:
                    routing_matrices()
                b = i - 3
                if 0 <= b < B:
                    dve.wait_ge(hthi_ready, b + 1)
                    V.tensor_tensor(HTL[:, :, b * T:(b + 1) * T], TR[b % 2][:].rearrange("p (k t) -> p k t", k=H),
                                    HTH[:, :, b * T:(b + 1) * T].bitcast(f32), ALU.subtract).then_inc(htlo_ready, 1)

            dve.sem_inc(gu_free, 2)
            dve.sem_inc(actlo_done, 2)
            dve.sem_inc(act_used, ST)
            dve.sem_inc(down_read, TPC)
            dve.sem_inc(shared_added, 2)
            dve.wait_ge(logits_done, 1)
            V.tensor_scalar(KEY, LG[:, 0:T], TOP, BOTTOM, ALU.min, ALU.max).then_inc(key_ready, 1)
            dve.wait_ge(key_ready, 1)

            def count():
                for j in range(3):
                    V.tensor_scalar(reached[j], KEY, mids[:, j:j + 1], None, ALU.is_ge, ALU.add,
                                    accum_out=cntb[:, j:j + 1]).then_inc(counted, 1)

            def step(k, last=False):
                dve.wait_ge(totals, k + 1)
                V.tensor_scalar(geq[:], CNT[:, 0:3], float(CAP), None, ALU.is_ge, ALU.add, accum_out=s_).then_inc(step_order, 1)
                dve.wait_ge(step_order, 4 * k + 1)
                V.scalar_tensor_tensor(lo, s_, w, lo, ALU.mult, ALU.add).then_inc(step_order, 1)
                V.tensor_scalar(w, w, 0.25, None, ALU.mult).then_inc(step_order, 1)
                dve.wait_ge(step_order, 4 * k + 3)
                V.scalar_tensor_tensor(mids[:], iota3[:], w, lo.broadcast_to([P, 3]), ALU.mult, ALU.add).then_inc(step_order, 1)
                dve.wait_ge(step_order, 4 * k + 4)
                if not last:
                    count()

            reached = TMPA.bitcast(bf16)[:, 0:T], TMPA.bitcast(bf16)[:, T:2 * T], TMPB.bitcast(bf16)[:, 0:T]
            count()

            def glu(n, sg, u, af, bias=None):
                dve.wait_ge(silu_done, n + 1)
                dve.wait_ge(actlo_done, n + 1)
                if bias is None:
                    ins = V.tensor_tensor(af, u, sg, ALU.mult)
                else:
                    ins = V.scalar_tensor_tensor(af, u, bias, sg, ALU.add, ALU.mult)
                ins.then_inc(gu_free, 1)

            def act_lo(n, af, sl):
                dve.wait_ge(acthi_done, n + 1)
                V.tensor_tensor(AL[:, sl], af, AH[:, sl].bitcast(f32), ALU.subtract).then_inc(actlo_done, 1)

            def shared_glu(c, ft):
                glu(c * ST + ft, SG[ft % 2], PS[2 + ft % 2][:], AF[ft % 2])

            shared_glu(0, 0)
            with dve.Fori(0, NCH - 2) as c:
                def shared_step(k):
                    step(c * RPC + k)
                for k in range(RPC):
                    shared_step(k)
                    if k < ST - 1:
                        shared_glu(c, k + 1)
                shared_glu(c + 1, 0)
            for k in range(RPC * (NCH - 2), ROUNDS):
                step(k, last=(k == ROUNDS - 1))
                if k < ROUNDS - 1:
                    shared_glu(NCH - 2, k - RPC * (NCH - 2) + 1)

            hi = four_w
            c_hi, c_ge, off1, off2 = cntb[:, 1:2], cntb[:, 2:3], small[:, 4:5], small[:, 5:6]
            mark(V.scalar_tensor_tensor(hi, w, 4.0, lo, ALU.mult, ALU.add))
            mark(V.tensor_scalar(MHI, KEY, lo, None, ALU.is_gt))
            dve.wait_ge(dve_order, n[0])
            link(V.tensor_scalar(TMPB, KEY, hi, None, ALU.is_ge))
            mark(V.tensor_tensor(MHI, MHI, TMPB, ALU.mult))
            link(V.tensor_scalar(MGE, KEY, lo, None, ALU.is_ge, ALU.add, accum_out=c_ge))
            mark(V.tensor_scalar(TMPA, MHI, 1.0, None, ALU.mult, ALU.add, accum_out=c_hi))
            V.memset(TMPB, 1.0).then_inc(tails, 1)
            dve.wait_ge(tails, 1)
            dve.wait_ge(dve_order, n[0])
            mark(V.tensor_tensor_scan(PHI, TMPB, MHI, 0.0, ALU.mult, ALU.add))
            mark(V.tensor_tensor_scan(PGE, TMPB, MGE, 0.0, ALU.mult, ALU.add))
            dve.wait_ge(tail_tot, 1)
            link(V.tensor_copy(small[:, 5:8], CNT[:, 0:3]))
            link(V.scalar_tensor_tensor(off1, small[:, 6:7], 1.0, small[:, 5:6], ALU.mult, ALU.subtract))
            link(V.tensor_tensor(off1, off1, small[:, 7:8], ALU.add))
            link(V.scalar_tensor_tensor(TMPA, PGE, off1, PHI, ALU.add, ALU.subtract))
            link(V.scalar_tensor_tensor(TMPB, PHI, small[:, 5:6], TMPA, ALU.add, ALU.subtract))
            mark(V.tensor_tensor(TMPB, TMPB, MHI, ALU.mult))
            link(V.tensor_tensor(TMPA, TMPA, MGE, ALU.mult))
            V.tensor_tensor(TMPA, TMPA, TMPB, ALU.add).then_inc(slots_ready, 1)
            shared_glu(NCH - 1, 0)
            slt = SLT.rearrange("p (b j e) -> p b j e", j=2, e=NE)
            for j in range(2):
                dve.wait_ge(slots_turned, 2)
                mark(V.tensor_copy(slt[:, :, j, :], PS[6][:, j * P:(j + 1) * P].rearrange("p (b e) -> p b e", e=NE)))
            dve.wait_ge(dve_order, n[0])
            si, si2 = SINT.bitcast(i32), SINT2.bitcast(i32)
            link(V.tensor_scalar(si, SLT, -1.0, None, ALU.add))
            mark(V.tensor_scalar(si2, si, 4, None, ALU.arith_shift_right))
            link(V.tensor_scalar(si, si, 15, None, ALU.bitwise_and))
            mark(V.tensor_copy(SHIF, si2))
            link(V.tensor_copy(SLOF, si))
            oa = OA.rearrange("p (tg s e) -> p s tg e", s=16, e=8)
            ob = OB.rearrange("p (s n) -> p s n", s=16)

            def one_hot(dst, digit):
                for s in range(16):
                    mark(V.tensor_scalar(dst[:, s], digit, float(s), None, ALU.is_equal))
            one_hot(oa, SHIF.rearrange("p (tg e) -> p tg e", e=8))
            shared_glu(NCH - 1, 1)
            one_hot(ob, SLOF)
            shared_glu(NCH - 1, 2)
            dve.wait_ge(dve_order, n[0])
            V.tensor_tensor(ob, ob, TIDS.unsqueeze(1).broadcast_to([P, 16, NT * NE]), ALU.mult).then_inc(onehots, 1)
            shared_glu(NCH - 1, 3)
            dve.wait_ge(ids_done, 1)
            V.tensor_tensor(IDH.rearrange("p (g n) -> p g n", g=2), PS[7][:, 0:2 * P].rearrange("p (g n) -> p g n", g=2),
                            own_block[:].unsqueeze(1).broadcast_to([P, 2, P]), ALU.mult).then_inc(ids_masked, 1)
            dve.wait_ge(ids_spread, 1)
            link(V.tensor_tensor(IDM.rearrange("p (g s e) -> p g s e", g=2, s=16), PS[6][:, 0:NE * 16].rearrange("p (g s e) -> p g s e", g=2, s=16),
                                 pick[:].rearrange("p j r -> p (j r)").unsqueeze(1).unsqueeze(3).broadcast_to([P, 2, 16, 8]), ALU.mult))
            for g in range(2):
                mark(V.tensor_reduce(IDR[:, g * 16:(g + 1) * 16].rearrange("p (e j) -> p e j", j=2),
                                     IDM[:, g * P:(g + 1) * P].rearrange("p (j r e) -> p e j r", j=2, r=8), AX.X, ALU.add))
            dve.wait_ge(dve_order, n[0])
            V.tensor_copy(IDXALL[:].rearrange("p e j -> p (e j)"), IDR).then_inc(idx_ready, 1)

            def xt_lo(e):
                dve.wait_ge(xthi_done, e + 1)
                V.tensor_tensor(XTL[:], PS[6][:].rearrange("p (k t) -> p k t", k=H), XTH[:].bitcast(f32), ALU.subtract).then_inc(xtlo_done, 1)

            xt_lo(0)
            for q in range(SBASE, GUP):
                split_weight(SPIECES + q + 1, q, raw_of(q))

            def expert(e, s, first=False, last=False):
                def next_lo(q):
                    if not last:
                        split_weight(SPIECES + NP * (e + 1) + (q + 1), q, raw_of(q))

                def lo_of(f):
                    act_lo(SN + FT * e + f, AF[f % 2][:, 0:CAP], slice(f * CAP, (f + 1) * CAP))
                for f in range(FT):
                    glu(SN + FT * e + f, SG[f % 2][:, 0:CAP], PS[f % 4][:, CAP:2 * CAP], AF[f % 2][:, 0:CAP],
                        bias=FB[s][:, FT + f:FT + f + 1])
                    if f >= 1:
                        lo_of(f - 1)
                        next_lo(f - 1)
                lo_of(FT - 1)
                next_lo(GUP - 1)
                if not last:
                    xt_lo(e + 1)
                dve.wait_ge(act_used, ST + SN + FT * e + FT)
                dve.wait_ge(db_arrived[s], 8 * (e - s) + 16)
                if not first:
                    dve.wait_ge(y_ready, 2 * e)
                for j in range(2):
                    V.tensor_tensor(Y[s][:, j * C:(j + 1) * C], OUT[j][:, 0:C], DB[s], ALU.add).then_inc(y_biased, 1)

            expert(0, 0, first=True)
            with dve.Fori(0, (NE - 2) // 2) as pair:
                for s in range(2):
                    expert(pair * 2 + (s + 1), 1 - s)
            expert(NE - 1, 1, last=True)

        @block.tensor
        def _(pe):
            M = nc.tensor.matmul

            def three(dst, lhs, rhs, start, stop, **kw):
                (lh, ll), (rh, rl) = lhs, rhs
                M(dst, lh, rh, start=start, stop=False, **kw)
                M(dst, lh, rl, start=False, stop=False, **kw)
                return M(dst, ll, rh, start=False, stop=stop, **kw)

            pe.wait_ge(den_consts, H)
            def gate_up(c, ft, after_half=None):
                piece = SBASE + ft
                for g, bank in ((0, ft % 2), (1, 2 + ft % 2)):
                    for k in range(H):
                        sl = slice(g * 2 * P + k * P, g * 2 * P + (k + 1) * P)
                        last = three(PS[bank][:], (WH[:, piece, sl], WL[:, piece, sl]),
                                     (HTH[:, k, bass.ds(c * CT, CT)], HTL[:, k, bass.ds(c * CT, CT)]),
                                     start=(k == 0), stop=(k == H - 1))
                        if g == 1 and k == H - 1:
                            last.then_inc(gu_done, 1)
                        if after_half:
                            after_half()

            for i in range(B + 4):
                b = i - 4
                if 0 <= b < B:
                    pe.wait_ge(htlo_ready, b + 1)
                    sl = slice(b * T, (b + 1) * T)
                    win = slice(GSTRIP - NE * b, GSTRIP - NE * b + P)
                    for k in range(H):
                        last = three(LG[:, 0:T], (GWH[:, k, win], GWL[:, k, win]), (HTH[:, k, sl], HTL[:, k, sl]),
                                     start=(b == 0 and k == 0), stop=(b == B - 1 and k == H - 1))
                    if b == B - 1:
                        last.then_inc(logits_done, 1)
                b = i - 3
                if 0 <= b < B:
                    pe.wait_ge(h_ready, 2 * b + 2)
                    if b >= 2:
                        pe.wait_ge(htlo_ready, b - 1)
                    for k in range(H):
                        for th in range(2):
                            last = nc.tensor.transpose(TR[b % 2][:, k * T + th * P:k * T + (th + 1) * P],
                                                       HB[b % 2][:, th, k * P:(k + 1) * P], ident[:])
                    last.then_inc(ht_ready, 1)
                if i == B + 1:
                    pe.wait_ge(w0_lo, 1)
                    pe.wait_ge(htlo_ready, CT // T)
                    pe.wait_ge(t_ready, B - 1)
                    pe.wait_ge(q_ready, B - 1)
                    gate_up(0, 0)
                b = i
                if b < B:
                    s = b % 2
                    for dst, fw, own, bw, one, dg, scans, read, done in (
                            (DEN[s], SB_[s], EK[s], RB[s], ident[:], diag, 2, q_ready, den_done),
                            (NUM[s], SA[s], KV[s], RA[s], identg[:], diagg, 4, t_ready, num_done)):
                        if b == 0 and scans == 4:
                            pe.wait_ge(num_consts, 1 + H)
                        pe.wait_ge(scans_done, 4 * b + scans)
                        if b >= 2:
                            pe.wait_ge(read, b - 1)
                        for th in range(2):
                            for h in range(H):
                                at = h * SEG + th * P
                                o = dst[:, th * C + h * P:th * C + (h + 1) * P]
                                M(o, fw[:, at:at + P], one, start=True, stop=False)
                                M(o, bw[:, at + 2:at + 2 + P], one, start=False, stop=False)
                                last = M(o, own[:, at + 1:at + 1 + P], dg[:, h, :], start=False, stop=True)
                        last.then_inc(done, 1)

            def total(k):
                pe.wait_ge(counted, 3 * k + 3)
                M(CNT[:, 0:3], same[:], cntb[:, 0:3], start=True, stop=True).then_inc(totals, 1)

            pe.wait_ge(w0_lo, SPIECES)
            pe.wait_ge(htlo_ready, B)

            def chunk(c, between, last_one=False):
                part = [0]

                def next_part():
                    between(part[0])
                    part[0] += 1

                def down(ft):
                    pe.wait_ge(actlo_done, c * ST + (ft + 3))
                    piece, half = SBASE + ST + ft // 2, ft % 2
                    sl = slice(half * C, (half + 1) * C)
                    for tt in range(TPC):
                        a = slice(ft * CT + tt * P, ft * CT + (tt + 1) * P)
                        last = three(OUT[tt // 2][:, tt % 2 * C:(tt % 2 + 1) * C], (AH[:, a], AL[:, a]),
                                     (WH[:, piece, sl], WL[:, piece, sl]), start=(ft == 0 and tt % 2 == 0),
                                     stop=(ft == ST - 1), skip_group_check=True)
                        if tt == TPC - 1:
                            last.then_inc(act_used, 1)
                        if tt % 2 == 1:
                            next_part()

                for ft in range(1, ST):
                    pe.wait_ge(gu_free, c * ST + (ft + 1))
                    gate_up(c, ft, next_part)
                pe.wait_ge(down_read, c * TPC + TPC)
                for ft in range(ST - 1):
                    down(ft)
                if not last_one:
                    pe.wait_ge(gu_free, c * ST + (ST + 1))
                    gate_up(c + 1, 0, next_part)
                down(ST - 1)

            PARTS = 24
            def round_total(c, n):
                if n % (PARTS // RPC) == 2:
                    total(c * RPC + n // (PARTS // RPC))

            with pe.Fori(0, NCH - 2) as c:
                chunk(c, lambda n: round_total(c, n))
            pe.wait_ge(scores_ready, 1)
            for j in range(2):
                nc.tensor.transpose(PS[6][:, j * P:(j + 1) * P], SCO[:, j * P:(j + 1) * P], ident[:]).then_inc(scores_turned, 1)

            def offsets_and_slots(n):
                if n < (ROUNDS - RPC * (NCH - 2)) * (PARTS // RPC):
                    round_total(NCH - 2, n)
                if n == 19:
                    pe.wait_ge(tails, 1)
                    M(CNT[:, 0:2], before[:], cntb[:, 1:3], start=True, stop=True)
                    M(CNT[:, 2:3], same[:], cntb[:, 1:2], start=True, stop=True).then_inc(tail_tot, 1)
                if n == 23:
                    pe.wait_ge(slots_ready, 1)
                    pe.wait_ge(scores_laid, 2)
                    for j in range(2):
                        nc.tensor.transpose(PS[6][:, j * P:(j + 1) * P], TMPA[:, j * P:(j + 1) * P], ident[:]).then_inc(slots_turned, 1)

            def token_numbers(n):
                if n == 14:
                    pe.wait_ge(onehots, 1)
                    ob = OB.rearrange("p (s t e) -> p s t e", s=16, e=NE)
                    for t in range(NT):
                        for g in range(2):
                            last = M(PS[7][:, g * P:(g + 1) * P], OA[:, (2 * t + g) * P:(2 * t + g + 1) * P], ob[:, :, t, g * 8:g * 8 + 8],
                                     start=(t == 0 and g == 0), stop=(t == NT - 1), skip_group_check=True)
                    last.then_inc(ids_done, 1)
                if n == 16:
                    pe.wait_ge(ids_masked, 1)
                    M(PS[6][:, 0:2 * P], spread[:], IDH, start=True, stop=True).then_inc(ids_spread, 1)

            chunk(NCH - 2, offsets_and_slots)
            chunk(NCH - 1, token_numbers, last_one=True)
            def turn(e, s):
                pe.wait_ge(rows_gathered[s], 16 * (e - s) + 32)
                for k in range(H):
                    for j in range(2):
                        last = nc.tensor.transpose(PS[6][:, k * CAP + j * P:k * CAP + (j + 1) * P],
                                                   G[s][:, j * ROW + k * P:j * ROW + (k + 1) * P], ident[:])
                last.then_inc(xt_turned, 1)

            turn(0, 0)
            pe.wait_ge(gu_free, SN + 2)

            def expert(e, s, first=False, last_one=False):
                pe.wait_ge(xtlo_done, e + 1)
                for f in range(FT):
                    if first:
                        pe.wait_ge(*((w0_lo, SPIECES + (f + 1)) if f < SBASE else (w_lo, f + 1 - SBASE)))
                    else:
                        pe.wait_ge(w_lo, GUP * (e - 1) + (GUP - SBASE + f + 1))
                    pe.wait_ge(gu_free, SN + FT * e + (f - 1))
                    for g in range(2):
                        for k in range(H):
                            sl = slice(g * 2 * P + k * P, g * 2 * P + (k + 1) * P)
                            last = three(PS[f % 4][:, g * CAP:(g + 1) * CAP], (WH[:, f, sl], WL[:, f, sl]),
                                         (XTH[:, k, :], XTL[:, k, :]), start=(k == 0), stop=(k == H - 1))
                    last.then_inc(gu_done, 1)
                if first:
                    pe.wait_ge(down_read, TPC + NCH * TPC)
                else:
                    pe.wait_ge(y_biased, 2 * e)
                for k in range(FT):
                    if k == 2 and not last_one:
                        turn(e + 1, 1 - s)
                    pe.wait_ge(actlo_done, SN + FT * e + (k + 3))
                    if k % 2 == 0:
                        pe.wait_ge(wd_lo, DNP * e + (k // 2 + 1))
                    piece, sl = GUP + k // 2, slice(k % 2 * C, (k % 2 + 1) * C)
                    for j in range(2):
                        a = slice(k * CAP + j * P, k * CAP + (j + 1) * P)
                        last = three(OUT[j][:, 0:C], (AH[:, a], AL[:, a]), (WH[:, piece, sl], WL[:, piece, sl]),
                                     start=(k == 0), stop=(k == FT - 1))
                    last.then_inc(act_used, 1)

            expert(0, 0, first=True)
            with pe.Fori(0, (NE - 2) // 2) as pair:
                for s in range(2):
                    expert(pair * 2 + (s + 1), 1 - s)
            expert(NE - 1, 1, last_one=True)


def kernel(**inputs):
    import numpy as np
    import concourse.bacc as bacc
    from concourse import mybir
    from concourse.bass_utils import run_bass_kernel_spmd as run

    A = {k: np.asarray(v) for k, v in inputs.items()}
    P, E = 128, 16

    def gate_up(g, u):
        w = np.stack([g, u], axis=-3)
        lead = w.shape[:-3]
        w = w.reshape(*lead, 2, -1, P, 2, P)
        n = len(lead)
        w = w.transpose(*range(n), n + 4, n + 1, n, n + 3, n + 2)
        return np.ascontiguousarray(w.reshape(*lead, P, -1))

    def down(w):
        lead = w.shape[:-2]
        n = len(lead)
        w = w.reshape(*lead, 256, -1, P).transpose(*range(n), n + 2, n + 1, n)
        return np.ascontiguousarray(w.reshape(*lead, P, -1))

    halves = lambda v: v.reshape(2, P).T
    arrays = {
        "x": A["x"],
        "ctx": np.ascontiguousarray(A["ctx_1024"].transpose(2, 0, 1).reshape(2, P, 8, 256).transpose(1, 2, 0, 3)),
        "wu": np.ascontiguousarray(np.concatenate([halves(A["L0_xattn_w"].reshape(-1)), halves(A["L0_xattn_u"].reshape(-1))], axis=1)),
        "g": np.ascontiguousarray(np.broadcast_to(np.concatenate([A["g_xattn"], A["g_ffn"]]), (P, 2))),
        "gatew": np.ascontiguousarray(A["L0_ffn_gate_w"].reshape(E, 2, P).transpose(2, 1, 0)),
        "shgu": gate_up(A["L0_ffn_sh_gate_w"], A["L0_ffn_sh_up_w"]),
        "shd": down(A["L0_ffn_sh_down_w"]),
        "gu": gate_up(A["L0_ffn_gw"], A["L0_ffn_up_w"]),
        "dn": down(A["L0_ffn_down_w"]),
        "fb": np.ascontiguousarray(np.concatenate([A["L0_ffn_gb"].reshape(E, 8, P).transpose(0, 2, 1),
                                                   A["L0_ffn_up_b"].reshape(E, 8, P).transpose(0, 2, 1)], axis=2)),
        "db": A["L0_ffn_down_b"],
    }
    nc = bacc.Bacc("TRN2", target_bir_lowering=False, num_devices=1)
    aps = [nc.dram_tensor(f"in_{k}", a.shape, mybir.dt.from_np(a.dtype), kind="ExternalInput").ap() for k, a in arrays.items()]
    out = nc.dram_tensor("out_0", (8, 256, 256), mybir.dt.float32, kind="ExternalOutput").ap()
    flamingo_layer(nc, *aps, out)
    r = run(nc, [{f"in_{k}": a for k, a in arrays.items()}], core_ids=[0])
    return r.results[0]["out_0"]
```

```python
import concourse.bass as bass
from concourse import mybir
from contextlib import ExitStack


def flamingo_layer(nc, x_in, ctx_in, wu_in, g_in, gatew_in, shgu_in, shd_in, gu_in, dn_in, fb_in, db_in, out):
    f32, f32r, bf16, fp16 = mybir.dt.float32, mybir.dt.float32r, mybir.dt.bfloat16, mybir.dt.float16
    i32, u32 = mybir.dt.int32, mybir.dt.uint32
    ALU, ACT, AX = mybir.AluOpType, mybir.ActivationFunctionType, mybir.AxisListType

    P = 128
    B, T, C = 8, 256, 256
    H = C // P
    NT = B * T // P
    NE, F, SH = 16, 1024, 512
    CAP = B * T // NE * 2
    SEG = T + 1
    L = H * SEG + 1
    ROW = C + NE
    FT = F // P
    ST = SH // P
    PC = 512
    GUP, DNP = FT, FT * C // PC
    NP = GUP + DNP
    CT = 512
    NCH = B * T // CT
    TPC = CT // P
    ROUNDS = 16
    RPC = 6
    EPS = 1e-5
    TOP = 16.635532
    BOTTOM = -89.0
    LO0, W0 = -96.0, 32.0

    rows = nc.dram_tensor("h_rows", (B * T, ROW), f32, kind="Internal").ap()
    out_rows = out.rearrange("b t d -> (b t) d")

    with ExitStack() as ctx:
        def sb(name, shape, dt=f32):
            return ctx.enter_context(nc.sbuf_tensor(name, shape, dt))

        def sem(name):
            return ctx.enter_context(nc.semaphore(name))

        X = sb("X", [P, NT, C])
        WH = sb("WH", [P, NP, PC], f32r)
        WL = sb("WL", [P, NP, PC], f32r)
        RAWA = sb("RAWA", [P, 4 * PC])
        RAWB = sb("RAWB", [P, 4 * PC])
        RAWD = sb("RAWD", [P, 4 * PC])
        AH = sb("AH", [P, FT * CAP], f32r)
        AL = sb("AL", [P, FT * CAP], f32r)
        HTH = sb("HTH", [P, H, B * T], f32r)
        HTL = sb("HTL", [P, H, B * T], f32r)
        XTH = sb("XTH", [P, H, CAP], f32r)
        XTL = sb("XTL", [P, H, CAP], f32r)
        GSTRIP = P - NE
        GWH = sb("GWH", [P, H, GSTRIP + P], f32r)
        GWL = sb("GWL", [P, H, GSTRIP + P], f32r)
        GW = sb("GW", [P, H, GSTRIP + P])
        ident = sb("ident", [P, P])
        identg = sb("identg", [P, P])
        diag = sb("diag", [P, H, P])
        diagg = sb("diagg", [P, H, P])
        WU = sb("WU", [P, 2 * H])
        EWU = sb("EWU", [P, 2 * H])
        GIN = sb("GIN", [P, 2])
        TG = sb("TG", [P, 2])
        eps = sb("eps", [P, 1])
        D = sb("D", [P, L])
        KB = [sb(f"KB{s}", [P, H, T]) for s in range(4)]
        HB = [sb(f"HB{s}", [P, 2, C]) for s in range(2)]
        MV1 = sb("MV1", [P, NT, 2])
        NR1 = sb("NR1", [P, NT])
        BI1 = sb("BI1", [P, NT])
        R1 = sb("R1", [P, NT])
        MV2 = sb("MV2", [P, NT, 2])
        BS = sb("BS", [P, 2 * NT, 6])
        R2 = sb("R2", [P, NT])
        T2 = sb("T2", [P, NT])
        NB2 = sb("NB2", [P, NT])
        same = sb("same", [P, P], bf16)
        before = sb("before", [P, P], bf16)
        own_block = sb("own_block", [P, P])
        spread = sb("spread", [P, P], fp16)
        bitmat, rowmat = (KB[n][:, 0, 0:P].bitcast(i32) for n in range(2))
        masked, earlier = (KB[n][:, 1, 0:P] for n in range(2))
        TIDS = KB[2][:, 0, 0:P].bitcast(fp16)
        colnum = sb("colnum", [P, 1], i32)
        colf = sb("colf", [P, 1])
        iota3 = sb("iota3", [P, 3])
        pick = sb("pick", [P, 2, 8])
        IDXALL = sb("IDXALL", [P, NE, 2], u32)
        IDX = [sb(f"IDX{s}", [P, 2], u32) for s in range(2)]
        SIX = [sb(f"SIX{s}", [P, 2], u32) for s in range(2)]
        SCC = [sb(f"SCC{s}", [P, 2]) for s in range(2)]
        FB = [sb(f"FB{s}", [P, 2 * FT]) for s in range(2)]
        small = sb("small", [P, 16])
        mids = sb("mids", [P, 3])
        geq = sb("geq", [P, 3])
        cntb = sb("cntb", [P, 4], bf16)

        ARENA = 2 * 6 * L + 8 * 512
        AR = sb("AR", [P, ARENA])
        top = [0]

        def view(n, at=None):
            a = top[0] if at is None else at
            if at is None:
                top[0] += n
            assert a + n <= ARENA
            return AR[:, a:a + n]
        EK, KV, SA, RA, SB_, RB = [[view(L) for _ in range(2)] for _ in range(6)]
        E_, Q, RQ, TT = [[view(512) for _ in range(2)] for _ in range(4)]
        top[0] = 0
        SG = [view(512) for _ in range(2)]
        AF = [view(512) for _ in range(2)]
        KEY, MHI, MEQ, PHI, PEQ, SCO, TMPA, TMPB = [view(T) for _ in range(8)]
        SLT = view(NT * NE)
        SHIF, SLOF = [view(NT * NE // 2).bitcast(fp16) for _ in range(2)]
        SINT = view(NT * NE)
        SINT2 = view(NT * NE)
        SC = view(NT * NE)
        IDH = view(NE * 8).bitcast(fp16)
        IDM = PEQ
        IDR = view(NE * 2)
        SY = [view(C) for _ in range(2)]
        rest = top[0]
        OA = view(NT * NE * 8).bitcast(fp16)
        OB = view(NT * NE * 8).bitcast(fp16)
        top[0] = rest
        G = [view(2 * ROW) for _ in range(2)]
        Y = [view(2 * C) for _ in range(2)]
        DB = [view(C) for _ in range(2)]

        PS = [ctx.enter_context(nc.psum_tensor(f"PS{i}", [P, 512], f32)) for i in range(8)]
        NUM, DEN, TR, LG = PS[0:2], PS[2:4], PS[4:6], PS[6]
        OUT = PS[4:6]
        CNT = PS[7]

        wu_arrived, gates_arrived = sem("wu_arrived"), sem("gates_arrived")
        ctx_arrived = [sem(f"ctx_arrived{b}") for b in range(B)]
        x_arrived = [sem(f"x_arrived{b}") for b in range(B)]
        gw_arrived = sem("gw_arrived")
        rawa_arrived, rawb_arrived, rawd_arrived = sem("rawa_arrived"), sem("rawb_arrived"), sem("rawd_arrived")
        fb_arrived = [sem(f"fb_arrived{s}") for s in range(2)]
        db_arrived = [sem(f"db_arrived{s}") for s in range(2)]
        h_stored = [sem(f"h_stored{s}") for s in range(2)]
        scores_stored = sem("scores_stored")
        out_stored = sem("out_stored")
        pool_consts, routing_consts = sem("pool_consts"), sem("routing_consts")
        decay_exp, gates_tanh = sem("decay_exp"), sem("gates_tanh")
        dve_consts, den_consts, num_consts = sem("dve_consts"), sem("den_consts"), sem("num_consts")
        ln1_stats, ln1_rstd, ln1_affine = sem("ln1_stats"), sem("ln1_rstd"), sem("ln1_affine")
        act_order, dve_order, pool_order = sem("act_order"), sem("dve_order"), sem("pool_order")
        ek_ready, kv_ready, scans_done = sem("ek_ready"), sem("kv_ready"), sem("scans_done")
        den_done, num_done = sem("den_done"), sem("num_done")
        e_ready, q_ready, rq_ready, t_ready, x1_ready = sem("e_ready"), sem("q_ready"), sem("rq_ready"), sem("t_ready"), sem("x1_ready")
        ln2_stats, ln2_rstd, ln2_affine = sem("ln2_stats"), sem("ln2_rstd"), sem("ln2_affine")
        h_ready, ht_ready, hthi_ready, htlo_ready = sem("h_ready"), sem("ht_ready"), sem("hthi_ready"), sem("htlo_ready")
        logits_done = sem("logits_done")
        w_hi, w0_lo, w_lo, wd_lo = sem("w_hi"), sem("w0_lo"), sem("w_lo"), sem("wd_lo")
        key_ready, scores_ready, scores_turned, scores_laid = sem("key_ready"), sem("scores_ready"), sem("scores_turned"), sem("scores_laid")
        counted, totals = sem("counted"), sem("totals")
        step_order = sem("step_order")
        gu_done, silu_done, gu_free, banks_read = sem("gu_done"), sem("silu_done"), sem("gu_free"), sem("banks_read")
        acthi_done, actlo_done, act_used = sem("acthi_done"), sem("actlo_done"), sem("act_used")
        down_read, shared_added = sem("down_read"), sem("shared_added")
        last_down = sem("last_down")
        slots_turned, slots_ready, onehots, ids_done, idx_ready = sem("slots_turned"), sem("slots_ready"), sem("onehots"), sem("ids_done"), sem("idx_ready")
        ids_masked, ids_spread = sem("ids_masked"), sem("ids_spread")
        tails, tail_tot = sem("tails"), sem("tail_tot")
        rows_gathered = [sem(f"rows_gathered{s}") for s in range(2)]
        xt_turned, xthi_done, xtlo_done = sem("xt_turned"), sem("xthi_done"), sem("xtlo_done")
        y_biased, y_ready, scattered = sem("y_biased"), sem("y_ready"), sem("scattered")
        idx_copied = sem("idx_copied")
        kept, rows_known = sem("kept"), sem("rows_known")

        NPC = 4
        block = ctx.enter_context(nc.Block())

        SN = NCH * ST
        SPIECES = ST + ST * C // PC
        SBASE = GUP - 2

        def pick_expert(ap, e):
            if isinstance(e, int):
                return ap[e]
            return ap[bass.ds(e, 1), :, :].rearrange("o p n -> (o p) n")

        def raw_of(piece):
            return (RAWA, RAWB, RAWD)[piece // 4][:, piece % 4 * PC:(piece % 4 + 1) * PC]

        def raw_shared(piece):
            return RAWA[:, piece * PC:(piece + 1) * PC] if piece < ST else RAWB[:, (piece - ST) * PC:(piece - ST + 1) * PC]

        def tokens(t):
            return t[:, 1:1 + H * SEG].rearrange("p (h t) -> p h t", h=H)[:, :, 0:T]

        @block.sync
        def _(sp):
            sp.dma_start(WU[:], wu_in).then_inc(wu_arrived, 16)

            def load_batch(b):
                if b >= 4:
                    sp.wait_ge(kv_ready, b - 3)
                sp.dma_start(KB[b % 4][:], ctx_in[:, b, :, :]).then_inc(ctx_arrived[b], 16)
                sp.dma_start(X[:, 2 * b:2 * b + 2, :], x_in[b].rearrange("(i p) d -> p i d", p=P)).then_inc(x_arrived[b], 16)
            load_batch(0)
            sp.dma_start(GIN[:], g_in).then_inc(gates_arrived, 16)
            for b in range(1, 4):
                load_batch(b)
            sp.dma_start(RAWA[:], shgu_in).then_inc(rawa_arrived, 16)
            sp.dma_start(RAWB[:, 0:ST * C], shd_in).then_inc(rawb_arrived, 16)
            sp.wait_ge(dve_consts, 1)
            sp.dma_start(GW[:, :, GSTRIP:GSTRIP + NE], gatew_in).then_inc(gw_arrived, 16)
            for b in range(4, B):
                load_batch(b)
            sp.dma_start(RAWD[:], dn_in[0]).then_inc(rawd_arrived, 16)
            for b in range(B):
                sp.wait_ge(h_ready, 2 * (b + 1))
                sp.dma_start(rows[b * T:(b + 1) * T, 0:C].rearrange("(i p) d -> p i d", p=P), HB[b % 2][:]).then_inc(h_stored[b % 2], 16)
            sp.wait_ge(w0_lo, ST)
            sp.dma_start(RAWA[:], gu_in[0, :, 0:4 * PC]).then_inc(rawa_arrived, 16)
            sp.wait_ge(w0_lo, SPIECES)
            sp.dma_start(RAWB[:], gu_in[0, :, 4 * PC:8 * PC]).then_inc(rawb_arrived, 16)
            sp.dma_start(FB[0][:], fb_in[0]).then_inc(fb_arrived[0], 16)
            out_chunks = out_rows.rearrange("(c i p) d -> c p i d", p=P, i=TPC)

            def store_shared(c):
                sp.wait_ge(shared_added, TPC * c + (TPC + 2))
                dst = out_chunks[c] if isinstance(c, int) else out_chunks[bass.ds(c, 1), :, :, :].rearrange("o p i d -> (o p) i d")
                sp.dma_start(dst, X[:, bass.ds(c * TPC, TPC), :]).then_inc(out_stored, 16)

            with sp.Fori(0, NCH - 2) as c:
                store_shared(c)
            sp.wait_ge(scores_laid, 2)
            sp.dma_start(rows[:, C:ROW].rearrange("(i p) e -> p i e", p=P), SC.rearrange("p (i e) -> p i e", e=NE)).then_inc(scores_stored, 16)
            store_shared(NCH - 2)
            sp.wait_ge(idx_ready, 1)
            sp.dma_start(DB[0][:], db_in[0:1, :].rearrange("o d -> (o d)").partition_broadcast(P)).then_inc(db_arrived[0], 16)

            def load_first_pieces(e):
                sp.wait_ge(w_lo, GUP * (e - 1) + 4)
                sp.dma_start(RAWA[:], pick_expert(gu_in, e)[:, 0:4 * PC]).then_inc(rawa_arrived, 16)

            def load_rest(e, s, first=False):
                sp.wait_ge(w_lo, GUP * (e - 1) + 8)
                sp.dma_start(RAWB[:], pick_expert(gu_in, e)[:, 4 * PC:8 * PC]).then_inc(rawb_arrived, 16)
                sp.wait_ge(wd_lo, DNP * e)
                sp.dma_start(RAWD[:], pick_expert(dn_in, e)).then_inc(rawd_arrived, 16)
                if not first:
                    sp.wait_ge(y_biased, 2 * (e - 1))
                sp.dma_start(FB[s][:], pick_expert(fb_in, e)).then_inc(fb_arrived[s], 16)
                sp.dma_start(DB[s][:], (db_in[e:e + 1, :] if isinstance(e, int) else db_in[bass.ds(e, 1), :])
                             .rearrange("o d -> (o d)").partition_broadcast(P)).then_inc(db_arrived[s], 16)

            load_first_pieces(1)
            store_shared(NCH - 1)
            load_rest(1, 1, first=True)
            with sp.Fori(0, (NE - 2) // 2) as pair:
                for s in range(2):
                    load_first_pieces(pair * 2 + (s + 2))
                    load_rest(pair * 2 + (s + 2), s)
            sp.wait_ge(out_stored, 16 * NCH)
            sp.wait_ge(scattered, 32 * NE)
            sp.wait_ge(scores_stored, 16)
            for s in range(2):
                sp.wait_ge(h_stored[s], 16 * B // 2)

        @block.gpsimd
        def _(pool):
            nc.gpsimd.memset(ident[:], 0.0).then_inc(pool_order, 1)
            pool.wait_ge(pool_order, 1)
            nc.gpsimd.affine_select(out=ident[:], in_=ident[:], compare_op=ALU.not_equal, fill=1.0, base=0,
                                    pattern=[[-1, P]], channel_multiplier=1).then_inc(pool_consts, 1)
            n = [1]

            def mark(ins):
                n[0] += 1
                ins.then_inc(pool_order, 1)

            nc.gpsimd.iota(iota3[:], pattern=[[1, 3]], base=1, channel_multiplier=0,
                           allow_small_or_imprecise_dtypes=True).then_inc(pool_consts, 1)
            nc.gpsimd.iota(small[:, 8:16].bitcast(i32), pattern=[[1, 8]], base=P, channel_multiplier=-1).then_inc(pool_consts, 1)
            nc.gpsimd.iota(colnum[:], pattern=[[0, 1]], base=0, channel_multiplier=1).then_inc(pool_consts, 1)
            for s in range(2):
                for t in (EK[s], KV[s]):
                    mark(nc.gpsimd.memset(t[:, 0:L:SEG], 0.0))
            pads = n[0]

            def product(b):
                pool.wait_ge(pool_order, pads)
                if b >= 2:
                    pool.wait_ge(num_done, b - 1)
                pool.wait_ge(ek_ready, b + 1)
                nc.gpsimd.tensor_tensor(tokens(KV[b % 2]), tokens(EK[b % 2]), KB[b % 4][:], ALU.mult).then_inc(kv_ready, 1)

            def shared_weight_lo(q):
                pool.wait_ge(w_hi, q + 1)
                nc.gpsimd.tensor_tensor(WL[:, SBASE + q, :], raw_shared(q), WH[:, SBASE + q, :].bitcast(f32),
                                        ALU.subtract).then_inc(w0_lo, 1)

            product(0)
            for i in range(B + 3):
                b = i - 2
                if 0 <= b < B - 2:
                    pool.wait_ge(t_ready, b + 1)
                    pool.wait_ge(x_arrived[b], 16)
                    nc.gpsimd.tensor_tensor(X[:, 2 * b:2 * b + 2, :], X[:, 2 * b:2 * b + 2, :],
                                            TT[b % 2].rearrange("p (i c) -> p i c", i=2), ALU.add).then_inc(x1_ready, 1)
                if i + 1 < B:
                    product(i + 1)
                if 1 <= i <= SPIECES:
                    shared_weight_lo(i - 1)
                if i == B - 1:
                    nc.gpsimd.iota(bitmat, pattern=[[-1, P]], base=256, channel_multiplier=1).then_inc(routing_consts, 1)
                    nc.gpsimd.iota(rowmat, pattern=[[1, P]], base=0, channel_multiplier=0).then_inc(routing_consts, 1)
                    nc.gpsimd.iota(TIDS, pattern=[[P, NT], [0, NE]], base=0, channel_multiplier=1,
                                   allow_small_or_imprecise_dtypes=True).then_inc(routing_consts, 1)

            def wait_all(*waits):
                counts = [v if isinstance(v, int) else pool.to_reg(v) for _, v in waits]
                pool.wait_ge(pool_consts, NPC)
                for (signal, _), count in zip(waits, counts):
                    pool.wait_ge(signal, count)

            def act_lo(c, ft):
                sl = slice(ft * CT, (ft + 1) * CT)
                wait_all((acthi_done, c * ST + (ft + 1)))
                nc.gpsimd.tensor_tensor(AL[:, sl], AF[ft % 2], AH[:, sl].bitcast(f32), ALU.subtract).then_inc(actlo_done, 1)

            def add_shared(c):
                for tt in range(TPC):
                    wait_all((down_read, TPC + c * TPC + (tt + 1)))
                    xs = X[:, c * TPC + tt, :] if isinstance(c, int) else X[:, bass.ds(c * TPC + tt, 1), :].rearrange("p o d -> p (o d)")
                    nc.gpsimd.tensor_tensor(xs, xs, SY[tt % 2], ALU.add).then_inc(shared_added, 1)

            def glu(ft):
                pool.wait_ge(banks_read, ft + 1)
                nc.gpsimd.tensor_tensor(AF[ft % 2], AF[ft % 2], SG[ft % 2], ALU.mult).then_inc(gu_free, 1)

            with pool.Fori(0, NCH - 2) as c:
                for ft in range(ST):
                    act_lo(c, ft)
                add_shared(c)
            for ft in range(ST):
                act_lo(NCH - 2, ft)
            glu(0)
            add_shared(NCH - 2)
            glu(1)
            act_lo(NCH - 1, 0)
            glu(2)
            act_lo(NCH - 1, 1)
            act_lo(NCH - 1, 2)

            def fetch(e, s):
                at = IDX[s]
                if isinstance(e, int) and e == 0:
                    at = IDXALL[:, 0, :]
                else:
                    nc.gpsimd.tensor_copy(at[:], index_of(e)).then_inc(idx_copied, 1)
                    wait_all((idx_copied, e))
                for j in range(2):
                    pool.indirect_dma_start(G[s][:, j * ROW:(j + 1) * ROW], None, rows,
                                            bass.IndirectOffsetOnAxis(ap=at[:, j:j + 1], axis=0)).then_inc(rows_gathered[s], 16)

            def index_of(e):
                return IDXALL[:, e, :] if isinstance(e, int) else IDXALL[:, bass.ds(e, 1), :].rearrange("p o j -> p (o j)")

            def keep_scores(e, s):
                sc = G[s][:, C + e:C + e + ROW + 1:ROW] if isinstance(e, int) else G[s][:, bass.ds(e + C, 2, step=ROW)]
                wait_all((rows_gathered[s], 16 * (e - s) + 32))
                nc.gpsimd.tensor_copy(SCC[s][:], sc).then_inc(kept, 1)

            def finish(e, s):
                before_it = (out_stored, 16 * NCH) if isinstance(e, int) and e == 0 else (scattered, 32 * e)
                wait_all(before_it)
                nc.gpsimd.tensor_copy(SIX[s][:], index_of(e)).then_inc(rows_known, 1)
                last = isinstance(e, int) and e == NE - 1

                def add_rows(j):
                    pool.indirect_dma_start(out_rows, bass.IndirectOffsetOnAxis(ap=SIX[s][:, j:j + 1], axis=0),
                                            Y[s][:, j * C:(j + 1) * C], None, compute_op=ALU.add).then_inc(scattered, 16)
                for j in range(2):
                    wait_all((kept, e + 1), (y_biased, 2 * e + (j + 1)))
                    nc.gpsimd.tensor_scalar(Y[s][:, j * C:(j + 1) * C], Y[s][:, j * C:(j + 1) * C],
                                            SCC[s][:, j:j + 1], TG[:, 1:2], ALU.mult, ALU.mult).then_inc(y_ready, 1)
                    if last:
                        wait_all((y_ready, 2 * e + (j + 1)), (rows_known, e + 1))
                        add_rows(j)
                if not last:
                    wait_all((y_ready, 2 * e + 2), (rows_known, e + 1))
                    for j in range(2):
                        add_rows(j)

            pool.wait_ge(idx_ready, 1)
            pool.wait_ge(scores_stored, 16)
            for s in range(2):
                pool.wait_ge(h_stored[s], 16 * B // 2)
            fetch(0, 0)
            add_shared(NCH - 1)

            def down_lo(e, q):
                wait_all((w_hi, SPIECES + NP * e + (GUP + q + 1)))
                nc.gpsimd.tensor_tensor(WL[:, GUP + q, :], RAWD[:, q * PC:(q + 1) * PC],
                                        WH[:, GUP + q, :].bitcast(f32), ALU.subtract).then_inc(wd_lo, 1)

            def expert(e, s, first=False, last=False):
                keep_scores(e, s)
                if not last:
                    fetch(e + 1, 1 - s)
                if not first:
                    finish(e - 1, 1 - s)
                else:
                    for q in range(DNP):
                        down_lo(0, q)
                if not last:
                    for q in range(DNP):
                        down_lo(e + 1, q)

            expert(0, 0, first=True)
            with pool.Fori(0, (NE - 2) // 2) as pair:
                for s in range(2):
                    expert(pair * 2 + (s + 1), 1 - s)
            expert(NE - 1, 1, last=True)
            finish(NE - 1, 1)

        @block.scalar
        def _(act):
            n = [0]

            def link(ins):
                n[0] += 1
                ins.then_inc(act_order, 1)
                act.wait_ge(act_order, n[0])

            nc.scalar.preload_act_table_set("natural_log_exp_and_others")
            act.wait_ge(wu_arrived, 16)
            nc.scalar.activation(EWU[:], WU[:], ACT.Exp).then_inc(decay_exp, 1)

            def exp_k(b):
                act.wait_ge(ctx_arrived[b], 16)
                if b >= 2:
                    act.wait_ge(den_done, b - 1)
                    act.wait_ge(kv_ready, b - 1)
                else:
                    act.wait_ge(pool_order, 5)
                nc.scalar.activation(tokens(EK[b % 2]), KB[b % 4][:], ACT.Exp).then_inc(ek_ready, 1)

            def ln1(g):
                act.wait_ge(ln1_stats, g + 1)
                a = slice(4 * g, 4 * g + 4)
                link(nc.scalar.activation(R1[:, a], MV1[:, a, 1], ACT.Ln, bias=eps[:, 0:1]))
                nc.scalar.activation(R1[:, a], R1[:, a], ACT.Exp, scale=-0.5).then_inc(ln1_rstd, 1)

            def hi_weight(piece, raw):
                nc.scalar.activation(WH[:, piece, :], raw, ACT.Copy).then_inc(w_hi, 1)

            exp_k(0)
            exp_k(1)
            act.wait_ge(gates_arrived, 16)
            nc.scalar.activation(TG[:], GIN[:], ACT.Tanh).then_inc(gates_tanh, 1)
            nc.scalar.preload_act_table_set("natural_log_exp_and_others")

            def write_h(b):
                act.wait_ge(ln2_affine, b + 1)
                if b >= 2:
                    act.wait_ge(ht_ready, b - 1)
                    act.wait_ge(h_stored[b % 2], 16 * (b // 2))
                for j in range(2):
                    t = 2 * b + j
                    nc.scalar.activation(HB[b % 2][:, j, :], X[:, t, :], ACT.Identity, scale=R2[:, t:t + 1],
                                         bias=NB2[:, t:t + 1]).then_inc(h_ready, 1)

            def ht_hi(b):
                act.wait_ge(ht_ready, b + 1)
                nc.scalar.activation(HTH[:, :, b * T:(b + 1) * T], TR[b % 2][:].rearrange("p (k t) -> p k t", k=H),
                                     ACT.Copy).then_inc(hthi_ready, 1)

            for i in range(B + 3):
                if 0 <= i - 3 < B - 1:
                    write_h(i - 3)
                if 2 <= i + 1 < B:
                    exp_k(i + 1)
                if i == 0:
                    act.wait_ge(dve_consts, 1)
                    ln1(0)
                if 0 <= i - 3 < B and i not in (B, B + 1):
                    ht_hi(i - 3)
                b = i
                if b < B:
                    act.wait_ge(ln1_affine, 1 + b // 2)
                    if b >= 2:
                        act.wait_ge(q_ready, b - 1)
                    for j in range(2):
                        t = 2 * b + j
                        nc.scalar.activation(E_[b % 2][:, j * C:(j + 1) * C], X[:, t, :], ACT.Exp, scale=NR1[:, t:t + 1],
                                             bias=BI1[:, t:t + 1]).then_inc(e_ready, 1)
                b, a = i - 1, slice(2 * (i - 2), 2 * (i - 2) + 2)
                norm = 0 <= i - 2 < B
                if 0 <= b < B:
                    act.wait_ge(q_ready, b + 1)
                    n[0] += 1
                    nc.scalar.activation(Q[b % 2], Q[b % 2], ACT.Ln).then_inc(act_order, 1)
                    log_q = n[0]
                if norm:
                    act.wait_ge(ln2_stats, i - 1)
                    n[0] += 1
                    nc.scalar.activation(R2[:, a], MV2[:, a, 1], ACT.Ln, bias=eps[:, 0:1]).then_inc(act_order, 1)
                    log_var = n[0]
                if 0 <= b < B:
                    act.wait_ge(act_order, log_q)
                    if b >= 2:
                        act.wait_ge(t_ready, b - 1)
                    nc.scalar.activation(RQ[b % 2], Q[b % 2], ACT.Exp, scale=-1.0).then_inc(rq_ready, 1)
                if norm:
                    act.wait_ge(act_order, log_var)
                    nc.scalar.activation(R2[:, a], R2[:, a], ACT.Exp, scale=-0.5).then_inc(ln2_rstd, 1)
                if i == B + 1:
                    write_h(B - 1)
                if i in (B, B + 1):
                    ht_hi(i - 3)
                if i % 2 == 1 and i + 1 < B:
                    ln1((i + 1) // 2)
                if 1 <= i <= SPIECES:
                    act.wait_ge(rawa_arrived if i <= ST else rawb_arrived, 16)
                    hi_weight(SBASE + i - 1, raw_shared(i - 1))

            act.wait_ge(key_ready, 1)
            nc.scalar.activation(SCO, LG[:, 0:T], ACT.Sigmoid).then_inc(scores_ready, 1)

            def first_hi(q):
                if q % 4 == 0:
                    act.wait_ge((rawa_arrived, rawb_arrived, rawd_arrived)[q // 4], (32, 32, 16)[q // 4])
                if q >= SBASE + ST:
                    act.wait_ge(act_used, SN + 2 * (q - SBASE - ST + 1))
                elif q >= SBASE:
                    act.wait_ge(gu_done, SN - ST + (q - SBASE + 1))
                hi_weight(q, raw_of(q))

            def act_silu(c, ft):
                act.wait_ge(gu_done, c * ST + (ft + 1))
                act.wait_ge(gu_free, c * ST + (ft + 1))
                nc.scalar.activation(SG[ft % 2], PS[ft % 2][:], ACT.Silu).then_inc(silu_done, 1)
                if isinstance(c, int) and c == NCH - 1 and ft < ST - 1:
                    act.wait_ge(actlo_done, c * ST + (ft + 1))
                    nc.scalar.activation(AF[ft % 2], PS[2 + ft % 2][:], ACT.Copy).then_inc(banks_read, 1)

            def xt_hi(e):
                act.wait_ge(xt_turned, e + 1)
                nc.scalar.activation(XTH[:], PS[6][:].rearrange("p (k t) -> p k t", k=H), ACT.Copy).then_inc(xthi_done, 1)

            def chunk(c, expert0=(), scores=False, last=False):
                pieces = list(expert0)

                def act_hi(ft):
                    act.wait_ge(gu_free, c * ST + (ft + 3))
                    act.wait_ge(act_used, c * ST + (ft + 1))
                    nc.scalar.activation(AH[:, ft * CT:(ft + 1) * CT], AF[ft % 2], ACT.Copy).then_inc(acthi_done, 1)
                if scores:
                    for j in range(2):
                        act.wait_ge(scores_turned, 2)
                        nc.scalar.activation(SC.rearrange("p (b j e) -> p b j e", j=2, e=NE)[:, :, j, :],
                                             PS[6][:, j * P:(j + 1) * P].rearrange("p (b e) -> p b e", e=NE), ACT.Copy).then_inc(scores_laid, 1)
                if last:
                    act_hi(0)
                for ft in range(1, ST):
                    act_silu(c, ft)
                    if not last:
                        act_hi(ft - 1)
                    if pieces:
                        first_hi(pieces.pop(0))
                    if last:
                        act_hi(ft)
                if not last:
                    act_hi(ST - 1)
                for q in pieces:
                    first_hi(q)
                if not last:
                    act_silu(c + 1, 0)
                if last:
                    xt_hi(0)
                act.wait_ge(act_used, ST + c * ST + ST)
                for tt in range(TPC):
                    act.wait_ge(shared_added, TPC * c + (tt + 1))
                    nc.scalar.activation(SY[tt % 2], OUT[tt // 2][:, tt % 2 * C:(tt % 2 + 1) * C], ACT.Copy,
                                         scale=TG[:, 1:2]).then_inc(down_read, 1)

            act_silu(0, 0)
            with act.Fori(0, NCH - 2) as c:
                chunk(c)
            chunk(NCH - 2, range(0, ST), scores=True)
            chunk(NCH - 1, range(ST, GUP), last=True)

            def expert(e, s, first=False, last=False):
                act.wait_ge(fb_arrived[s], 8 * (e - s) + 16)
                for f in range(FT):
                    act.wait_ge(gu_done, SN + FT * e + (f + 1))
                    act.wait_ge(gu_free, SN + FT * e + (f + 1))
                    nc.scalar.activation(SG[f % 2][:, 0:CAP], PS[f % 4][:, 0:CAP], ACT.Silu, bias=FB[s][:, f:f + 1]).then_inc(silu_done, 1)
                    if f >= 1:
                        hi_of(e, f - 1)
                    if first and f < 2:
                        for q in range(GUP + 2 * f, GUP + 2 * f + 2):
                            first_hi(q)
                    if f >= 1 and not last:
                        next_hi(e, f - 1)
                hi_of(e, FT - 1)
                if last:
                    return
                next_hi(e, GUP - 1)
                xt_hi(e + 1)
                for q in range(GUP, NP):
                    next_hi(e, q)

            def hi_of(e, f):
                act.wait_ge(gu_free, SN + FT * e + (f + 3))
                act.wait_ge(act_used, SN + FT * e + (f + 1 - FT + ST))
                nc.scalar.activation(AH[:, f * CAP:(f + 1) * CAP], AF[f % 2][:, 0:CAP], ACT.Copy).then_inc(acthi_done, 1)

            def next_hi(e, q):
                if q % 4 == 0:
                    if q < GUP:
                        act.wait_ge((rawa_arrived, rawb_arrived)[q // 4], 16 * e + 48)
                    else:
                        act.wait_ge(rawd_arrived, 16 * e + 32)
                if q < GUP:
                    act.wait_ge(gu_done, SN + FT * e + (q + 1))
                else:
                    act.wait_ge(act_used, ST + SN + FT * e + 2 * (q - GUP + 1))
                hi_weight(q, raw_of(q))

            expert(0, 0, first=True)
            with act.Fori(0, (NE - 2) // 2) as pair:
                for s in range(2):
                    expert(pair * 2 + (s + 1), 1 - s)
            expert(NE - 1, 1, last=True)

        @block.vector
        def _(dve):
            n = [0]

            def mark(ins):
                n[0] += 1
                ins.then_inc(dve_order, 1)

            def link(ins):
                mark(ins)
                dve.wait_ge(dve_order, n[0])

            V = nc.vector
            mark(V.memset(D[:], 1.0))
            mark(V.memset(eps[:], EPS))
            link(V.memset(GW[:], 0.0))
            V.memset(small[:, 0:1], LO0).then_inc(dve_consts, 1)
            dve.wait_ge(dve_consts, 1)
            dve.wait_ge(decay_exp, 1)
            for h in range(H):
                mark(V.tensor_scalar(D[:, h * SEG + 1:(h + 1) * SEG], D[:, h * SEG + 1:(h + 1) * SEG], EWU[:, h:h + 1], None, ALU.mult))
            link(V.memset(D[:, 0:L:SEG], 0.0))

            def ln1(g):
                for t in range(4 * g, 4 * g + 4):
                    dve.wait_ge(x_arrived[t // 2], 16)
                    mark(V.bn_stats(BS[:, t, :], X[:, t, :]))
                dve.wait_ge(dve_order, n[0])
                for t in range(4 * g, 4 * g + 4):
                    ins = V.bn_aggr(MV1[:, t, :], BS[:, t, :])
                    if t < 4 * g + 3:
                        mark(ins)
                    else:
                        ins.then_inc(ln1_stats, 1)

            def ln1_scale(g):
                a = slice(4 * g, 4 * g + 4)
                dve.wait_ge(ln1_rstd, g + 1)
                mark(V.tensor_scalar(NR1[:, a], R1[:, a], -1.0, None, ALU.mult))
                V.tensor_tensor(BI1[:, a], MV1[:, a, 0], R1[:, a], ALU.mult).then_inc(ln1_affine, 1)

            dve.wait_ge(pool_consts, NPC)
            for h in range(H):
                ins = V.tensor_scalar(diag[:, h, :], ident[:], EWU[:, H + h:H + h + 1], None, ALU.mult)
                ins.then_inc(den_consts, 1)

            def num_matrices():
                dve.wait_ge(gates_tanh, 1)
                V.tensor_scalar(identg[:], ident[:], TG[:, 0:1], None, ALU.mult).then_inc(num_consts, 1)
                dve.wait_ge(den_consts, H)
                for h in range(H):
                    V.tensor_scalar(diagg[:, h, :], diag[:, h, :], TG[:, 0:1], None, ALU.mult).then_inc(num_consts, 1)

            def split_weight(count, piece, raw):
                dve.wait_ge(w_hi, count)
                V.tensor_tensor(WL[:, piece, :], raw, WH[:, piece, :].bitcast(f32), ALU.subtract).then_inc(w_lo, 1)

            lo, w, s_, four_w = (small[:, k:k + 1] for k in range(4))

            def routing_matrices():
                dve.wait_ge(routing_consts, 3)
                mi = masked.bitcast(i32)
                link(V.tensor_scalar(mi, bitmat, 15, None, ALU.bitwise_and))
                mark(V.tensor_scalar(same[:], mi, 0.0, None, ALU.is_equal))
                link(V.tensor_scalar(earlier, bitmat, 256.0, None, ALU.is_lt))
                mark(V.tensor_tensor(before[:], same[:], earlier, ALU.mult))
                link(V.tensor_scalar(bitmat, bitmat, 7, None, ALU.bitwise_and))
                mark(V.tensor_scalar(own_block[:], bitmat, 0.0, None, ALU.is_equal))

            def slot_matrices():
                link(V.tensor_scalar(small[:, 8:16].bitcast(i32), small[:, 8:16].bitcast(i32), 7, None, ALU.bitwise_and))
                for j in range(2):
                    mark(V.tensor_scalar(pick[:, j, :], small[:, 8:16].bitcast(i32), 0.0, None, ALU.is_equal))
                mark(V.tensor_scalar(rowmat, rowmat, 3, None, ALU.arith_shift_right))
                link(V.tensor_scalar(colnum[:], colnum[:], 3, None, ALU.arith_shift_right))
                link(V.tensor_copy(colf[:], colnum[:]))
                mark(V.tensor_scalar(spread[:], rowmat, colf[:, 0:1], None, ALU.is_equal))
                mark(V.memset(w, W0))
                link(V.tensor_scalar(mids[:], iota3[:], W0, LO0, ALU.mult, ALU.add))

            def newton(b):
                a = slice(2 * b, 2 * b + 2)
                dve.wait_ge(ln2_rstd, b + 1)
                link(V.scalar_tensor_tensor(T2[:, a], MV2[:, a, 1], EPS, R2[:, a], ALU.add, ALU.mult))
                link(V.scalar_tensor_tensor(T2[:, a], T2[:, a], -0.5, R2[:, a], ALU.mult, ALU.mult))
                link(V.scalar_tensor_tensor(R2[:, a], T2[:, a], 1.5, R2[:, a], ALU.add, ALU.mult))
                V.scalar_tensor_tensor(NB2[:, a], MV2[:, a, 0], -1.0, R2[:, a], ALU.mult, ALU.mult).then_inc(ln2_affine, 1)

            def attended(b):
                dve.wait_ge(rq_ready, b + 1)
                dve.wait_ge(num_done, b + 1)
                if b >= 2:
                    dve.wait_ge(x1_ready, b - 1)
                V.tensor_tensor(TT[b % 2], NUM[b % 2][:], RQ[b % 2], ALU.mult).then_inc(t_ready, 1)

            def add_attended(b):
                dve.wait_ge(t_ready, b + 1)
                dve.wait_ge(x1_ready, b)
                V.tensor_tensor(X[:, 2 * b:2 * b + 2, :], X[:, 2 * b:2 * b + 2, :],
                                TT[b % 2].rearrange("p (i c) -> p i c", i=2), ALU.add).then_inc(x1_ready, 1)

            def ht_lo(b):
                dve.wait_ge(hthi_ready, b + 1)
                V.tensor_tensor(HTL[:, :, b * T:(b + 1) * T], TR[b % 2][:].rearrange("p (k t) -> p k t", k=H),
                                HTH[:, :, b * T:(b + 1) * T].bitcast(f32), ALU.subtract).then_inc(htlo_ready, 1)

            for i in range(B + 3):
                attended_first = i >= B or i % 2 == 1
                if 0 <= i - 2 < B and attended_first:
                    attended(i - 2)
                    if i == B:
                        add_attended(i - 2)
                if 0 <= i - 3 < B - 1:
                    newton(i - 3)
                if i == B + 1:
                    add_attended(i - 2)
                if i % 2 == 0 and 0 < i < B:
                    ln1_scale(i // 2)
                if 0 <= i - 2 < B and not attended_first:
                    attended(i - 2)
                b = i
                if b < B:
                    s = b % 2
                    if i == 0:
                        dve.wait_ge(dve_order, n[0])
                    if b >= 2:
                        dve.wait_ge(den_done, b - 1)
                    dve.wait_ge(ek_ready, b + 1)
                    V.tensor_tensor_scan(SB_[s], D[:], EK[s], 0.0, ALU.mult, ALU.add).then_inc(scans_done, 1)
                    V.tensor_tensor_scan(RB[s][:, ::-1], D[:, ::-1], EK[s][:, ::-1], 0.0, ALU.mult, ALU.add).then_inc(scans_done, 1)
                    if b >= 2:
                        dve.wait_ge(num_done, b - 1)
                    dve.wait_ge(kv_ready, b + 1)
                    V.tensor_tensor_scan(SA[s], D[:], KV[s], 0.0, ALU.mult, ALU.add).then_inc(scans_done, 1)
                    V.tensor_tensor_scan(RA[s][:, ::-1], D[:, ::-1], KV[s][:, ::-1], 0.0, ALU.mult, ALU.add).then_inc(scans_done, 1)
                if i == 0:
                    ln1(0)
                    num_matrices()
                if i == 1:
                    ln1_scale(0)
                    ln1(1)
                b = i - 2
                if 0 <= b < B:
                    dve.wait_ge(x1_ready, b + 1)
                    for j in range(2):
                        mark(V.bn_stats(BS[:, NT + 2 * b + j, :], X[:, 2 * b + j, :]))
                    stats_at = n[0]
                b = i - 1
                if 0 <= b < B:
                    dve.wait_ge(den_done, b + 1)
                    dve.wait_ge(e_ready, 2 * b + 2)
                    if b >= 2:
                        dve.wait_ge(rq_ready, b - 1)
                    V.scalar_tensor_tensor(Q[b % 2], E_[b % 2], 1.0, DEN[b % 2][:], ALU.add, ALU.mult).then_inc(q_ready, 1)
                if i == B + 1:
                    ht_lo(B - 3)
                b = i - 2
                if 0 <= b < B:
                    dve.wait_ge(dve_order, stats_at)
                    mark(V.bn_aggr(MV2[:, 2 * b, :], BS[:, NT + 2 * b, :]))
                    V.bn_aggr(MV2[:, 2 * b + 1, :], BS[:, NT + 2 * b + 1, :]).then_inc(ln2_stats, 1)
                    if b == 0:
                        dve.wait_ge(gw_arrived, 16)
                        link(V.tensor_copy(GWH[:], GW[:]))
                        mark(V.tensor_tensor(GWL[:], GW[:], GWH[:].bitcast(f32), ALU.subtract))
                if i % 2 == 1 and 1 < i < B - 1:
                    ln1((i + 1) // 2)
                if i == B:
                    routing_matrices()
                if i == B + 1:
                    newton(B - 1)
                    slot_matrices()
                if 0 <= i - 3 < B and i != B:
                    ht_lo(i - 3)

            ones = SLT
            mark(V.memset(ones, 1.0))
            dve.sem_inc(gu_free, 2)
            dve.sem_inc(actlo_done, 2)
            dve.sem_inc(act_used, ST)
            dve.sem_inc(down_read, TPC)
            dve.sem_inc(shared_added, 2)
            dve.wait_ge(logits_done, 1)
            V.tensor_scalar(KEY, LG[:, 0:T], TOP, BOTTOM, ALU.min, ALU.max).then_inc(key_ready, 1)
            dve.wait_ge(key_ready, 1)

            def count():
                for j in range(3):
                    V.tensor_scalar(reached[j], KEY, mids[:, j:j + 1], None, ALU.is_ge, ALU.add,
                                    accum_out=cntb[:, j:j + 1]).then_inc(counted, 1)

            def step(k, last=False):
                dve.wait_ge(totals, k + 1)
                V.tensor_scalar(geq[:], CNT[:, 0:3], float(CAP), None, ALU.is_ge, ALU.add, accum_out=s_).then_inc(step_order, 1)
                dve.wait_ge(step_order, 4 * k + 1)
                V.scalar_tensor_tensor(lo, s_, w, lo, ALU.mult, ALU.add).then_inc(step_order, 1)
                V.tensor_scalar(w, w, 0.25, None, ALU.mult).then_inc(step_order, 1)
                dve.wait_ge(step_order, 4 * k + 3)
                if last:
                    return
                V.scalar_tensor_tensor(mids[:], iota3[:], w, lo.broadcast_to([P, 3]), ALU.mult, ALU.add).then_inc(step_order, 1)
                dve.wait_ge(step_order, 4 * k + 4)
                count()

            reached = TMPA.bitcast(bf16)[:, 0:T], TMPA.bitcast(bf16)[:, T:2 * T], TMPB.bitcast(bf16)[:, 0:T]
            count()

            def glu(n, sg, u, af, bias=None):
                dve.wait_ge(silu_done, n + 1)
                dve.wait_ge(actlo_done, n + 1)
                if bias is None:
                    ins = V.tensor_tensor(af, u, sg, ALU.mult)
                else:
                    ins = V.scalar_tensor_tensor(af, u, bias, sg, ALU.add, ALU.mult)
                ins.then_inc(gu_free, 1)

            def act_lo(n, af, sl):
                dve.wait_ge(acthi_done, n + 1)
                V.tensor_tensor(AL[:, sl], af, AH[:, sl].bitcast(f32), ALU.subtract).then_inc(actlo_done, 1)

            def shared_glu(c, ft):
                glu(c * ST + ft, SG[ft % 2], PS[2 + ft % 2][:], AF[ft % 2])

            shared_glu(0, 0)
            with dve.Fori(0, NCH - 2) as c:
                for k in range(RPC):
                    step(c * RPC + k)
                    if k < ST - 1:
                        shared_glu(c, k + 1)
                shared_glu(c + 1, 0)
            for k in range(ROUNDS - RPC * (NCH - 2)):
                step(RPC * (NCH - 2) + k, last=(k == ROUNDS - RPC * (NCH - 2) - 1))
                if k < ST - 1:
                    shared_glu(NCH - 2, k + 1)

            hi = four_w
            c_hi, c_eq = cntb[:, 0:1], cntb[:, 1:2]
            link(V.scalar_tensor_tensor(hi, w, 4.0, lo, ALU.mult, ALU.add))
            link(V.tensor_scalar(TMPB, KEY, hi, None, ALU.is_ge))
            link(V.scalar_tensor_tensor(MHI, KEY, lo, TMPB, ALU.is_gt, ALU.mult, accum_out=c_hi))
            V.scalar_tensor_tensor(MEQ, KEY, lo, MHI, ALU.is_ge, ALU.subtract, accum_out=c_eq).then_inc(tails, 1)
            dve.wait_ge(tails, 1)
            mark(V.tensor_tensor_scan(PHI, ones, MHI, 0.0, ALU.mult, ALU.add))
            mark(V.tensor_tensor_scan(PEQ, ones, MEQ, 0.0, ALU.mult, ALU.add))
            dve.wait_ge(tail_tot, 1)
            link(V.tensor_copy(small[:, 4:6], CNT[:, 0:2]))
            mark(V.scalar_tensor_tensor(TMPA, PHI, small[:, 4:5], MHI, ALU.add, ALU.mult))
            link(V.scalar_tensor_tensor(TMPB, PEQ, small[:, 5:6], MEQ, ALU.add, ALU.mult))
            V.tensor_tensor(TMPA, TMPA, TMPB, ALU.add).then_inc(slots_ready, 1)
            si, si2 = SINT.bitcast(i32), SINT2.bitcast(i32)
            sit = si.rearrange("p (b j e) -> p b j e", j=2, e=NE)
            for j in range(2):
                dve.wait_ge(slots_turned, 2)
                mark(V.tensor_scalar(sit[:, :, j, :], PS[6][:, j * P:(j + 1) * P].rearrange("p (b e) -> p b e", e=NE), -1.0, None, ALU.add))
            dve.wait_ge(dve_order, n[0])
            mark(V.tensor_scalar(si2, si, 4, None, ALU.arith_shift_right))
            link(V.tensor_scalar(si, si, 15, None, ALU.bitwise_and))
            mark(V.tensor_copy(SHIF, si2))
            link(V.tensor_copy(SLOF, si))
            oa = OA.rearrange("p (tg s e) -> p s tg e", s=16, e=8)
            ob = OB.rearrange("p (s n) -> p s n", s=16)

            def one_hot(dst, digit):
                for s in range(16):
                    mark(V.tensor_scalar(dst[:, s], digit, float(s), None, ALU.is_equal))
            one_hot(oa, SHIF.rearrange("p (tg e) -> p tg e", e=8))
            one_hot(ob, SLOF)
            dve.wait_ge(dve_order, n[0])
            for half in range(2):
                a = slice(half * P, (half + 1) * P)
                V.tensor_tensor(ob[:, :, a], ob[:, :, a], TIDS[:, a].unsqueeze(1).broadcast_to([P, 16, P]), ALU.mult).then_inc(onehots, 1)
            dve.wait_ge(ids_done, 1)
            V.tensor_tensor(IDH.rearrange("p (g n) -> p g n", g=2), PS[7][:, 0:2 * P].rearrange("p (g n) -> p g n", g=2),
                            own_block[:].unsqueeze(1).broadcast_to([P, 2, P]), ALU.mult).then_inc(ids_masked, 1)
            dve.wait_ge(ids_spread, 1)
            link(V.tensor_tensor(IDM.rearrange("p (g s e) -> p g s e", g=2, s=16), PS[6][:, 0:NE * 16].rearrange("p (g s e) -> p g s e", g=2, s=16),
                                 pick[:].rearrange("p j r -> p (j r)").unsqueeze(1).unsqueeze(3).broadcast_to([P, 2, 16, 8]), ALU.mult))
            for g in range(2):
                mark(V.tensor_reduce(IDR[:, g * 16:(g + 1) * 16].rearrange("p (e j) -> p e j", j=2),
                                     IDM[:, g * P:(g + 1) * P].rearrange("p (j r e) -> p e j r", j=2, r=8), AX.X, ALU.add))
            dve.wait_ge(dve_order, n[0])
            V.tensor_copy(IDXALL[:].rearrange("p e j -> p (e j)"), IDR).then_inc(idx_ready, 1)

            dve.wait_ge(gu_free, SN + 1)
            shared_glu(NCH - 1, ST - 1)
            dve.wait_ge(actlo_done, SN + 1)
            act_lo(SN - 1, AF[(ST - 1) % 2], slice((ST - 1) * CT, ST * CT))

            def xt_lo(e):
                dve.wait_ge(xthi_done, e + 1)
                V.tensor_tensor(XTL[:], PS[6][:].rearrange("p (k t) -> p k t", k=H), XTH[:].bitcast(f32), ALU.subtract).then_inc(xtlo_done, 1)

            for q in range(GUP):
                if q == ST:
                    xt_lo(0)
                split_weight(SPIECES + q + 1, q, raw_of(q))

            def expert(e, s, first=False, last=False):
                def next_lo(q):
                    if not last:
                        split_weight(SPIECES + NP * (e + 1) + (q + 1), q, raw_of(q))

                def lo_of(f):
                    act_lo(SN + FT * e + f, AF[f % 2][:, 0:CAP], slice(f * CAP, (f + 1) * CAP))
                for f in range(FT):
                    glu(SN + FT * e + f, SG[f % 2][:, 0:CAP], PS[f % 4][:, CAP:2 * CAP], AF[f % 2][:, 0:CAP],
                        bias=FB[s][:, FT + f:FT + f + 1])
                    if f >= 1:
                        lo_of(f - 1)
                        next_lo(f - 1)
                lo_of(FT - 1)
                next_lo(GUP - 1)
                if not last:
                    xt_lo(e + 1)
                if not last:
                    dve.wait_ge(act_used, ST + SN + FT * e + FT)
                dve.wait_ge(db_arrived[s], 8 * (e - s) + 16)
                if not first:
                    dve.wait_ge(y_ready, 2 * e)
                for j in range(2):
                    if last:
                        dve.wait_ge(last_down, j + 1)
                    V.tensor_tensor(Y[s][:, j * C:(j + 1) * C], OUT[j][:, 0:C], DB[s], ALU.add).then_inc(y_biased, 1)

            expert(0, 0, first=True)
            with dve.Fori(0, (NE - 2) // 2) as pair:
                for s in range(2):
                    expert(pair * 2 + (s + 1), 1 - s)
            expert(NE - 1, 1, last=True)

        @block.tensor
        def _(pe):
            M = nc.tensor.matmul

            def three(dst, lhs, rhs, start, stop, **kw):
                (lh, ll), (rh, rl) = lhs, rhs
                M(dst, lh, rh, start=start, stop=False, **kw)
                M(dst, lh, rl, start=False, stop=False, **kw)
                return M(dst, ll, rh, start=False, stop=stop, **kw)

            pe.wait_ge(den_consts, H)
            def gate_up(c, ft, after_half=None, parts=(0, 1)):
                piece = SBASE + ft
                for g in parts:
                    bank = 2 * g + ft % 2
                    for k in range(H):
                        sl = slice(g * 2 * P + k * P, g * 2 * P + (k + 1) * P)
                        last = three(PS[bank][:], (WH[:, piece, sl], WL[:, piece, sl]),
                                     (HTH[:, k, bass.ds(c * CT, CT)], HTL[:, k, bass.ds(c * CT, CT)]),
                                     start=(k == 0), stop=(k == H - 1))
                        if g == 1 and k == H - 1:
                            last.then_inc(gu_done, 1)
                        if after_half:
                            after_half()

            def logits(b):
                pe.wait_ge(htlo_ready, b + 1)
                sl = slice(b * T, (b + 1) * T)
                win = slice(GSTRIP - NE * b, GSTRIP - NE * b + P)
                for k in range(H):
                    last = three(LG[:, 0:T], (GWH[:, k, win], GWL[:, k, win]), (HTH[:, k, sl], HTL[:, k, sl]),
                                 start=(b == 0 and k == 0), stop=(b == B - 1 and k == H - 1))
                if b == B - 1:
                    last.then_inc(logits_done, 1)

            for i in range(B + 4):
                if i == B + 1:
                    pe.wait_ge(w0_lo, 1)
                    pe.wait_ge(htlo_ready, CT // T)
                    pe.wait_ge(t_ready, B - 1)
                    pe.wait_ge(q_ready, B - 1)
                    gate_up(0, 0, parts=(0,))
                if 4 <= i < B + 1:
                    logits(i - 4)
                b = i - 3
                if 0 <= b < B:
                    pe.wait_ge(h_ready, 2 * b + 2)
                    if b >= 2:
                        pe.wait_ge(htlo_ready, b - 1)
                    for k in range(H):
                        for th in range(2):
                            last = nc.tensor.transpose(TR[b % 2][:, k * T + th * P:k * T + (th + 1) * P],
                                                       HB[b % 2][:, th, k * P:(k + 1) * P], ident[:])
                    last.then_inc(ht_ready, 1)
                if i == B + 1:
                    gate_up(0, 0, parts=(1,))
                if i >= B + 1:
                    logits(i - 4)
                b = i
                if b < B:
                    s = b % 2
                    for dst, fw, own, bw, one, dg, scans, read, done in (
                            (DEN[s], SB_[s], EK[s], RB[s], ident[:], diag, 2, q_ready, den_done),
                            (NUM[s], SA[s], KV[s], RA[s], identg[:], diagg, 4, t_ready, num_done)):
                        if b == 0 and scans == 4:
                            pe.wait_ge(num_consts, 1 + H)
                        pe.wait_ge(scans_done, 4 * b + scans)
                        if b >= 2:
                            pe.wait_ge(read, b - 1)
                        for th in range(2):
                            for h in range(H):
                                at = h * SEG + th * P
                                o = dst[:, th * C + h * P:th * C + (h + 1) * P]
                                M(o, fw[:, at:at + P], one, start=True, stop=False)
                                M(o, bw[:, at + 2:at + 2 + P], one, start=False, stop=False)
                                last = M(o, own[:, at + 1:at + 1 + P], dg[:, h, :], start=False, stop=True)
                        last.then_inc(done, 1)

            def total(k):
                pe.wait_ge(counted, 3 * k + 3)
                M(CNT[:, 0:3], same[:], cntb[:, 0:3], start=True, stop=True).then_inc(totals, 1)

            pe.wait_ge(w0_lo, SPIECES)
            pe.wait_ge(htlo_ready, B)

            def turn(e, s):
                pe.wait_ge(rows_gathered[s], 16 * (e - s) + 32)
                for k in range(H):
                    for j in range(2):
                        last = nc.tensor.transpose(PS[6][:, k * CAP + j * P:k * CAP + (j + 1) * P],
                                                   G[s][:, j * ROW + k * P:j * ROW + (k + 1) * P], ident[:])
                last.then_inc(xt_turned, 1)

            def chunk(c, between, last_one=False):
                part = [0]

                def next_part():
                    between(part[0])
                    part[0] += 1

                def down(ft):
                    pe.wait_ge(actlo_done, c * ST + (ft + 3))
                    piece, half = SBASE + ST + ft // 2, ft % 2
                    sl = slice(half * C, (half + 1) * C)
                    for tt in range(TPC):
                        a = slice(ft * CT + tt * P, ft * CT + (tt + 1) * P)
                        last = three(OUT[tt // 2][:, tt % 2 * C:(tt % 2 + 1) * C], (AH[:, a], AL[:, a]),
                                     (WH[:, piece, sl], WL[:, piece, sl]), start=(ft == 0 and tt % 2 == 0),
                                     stop=(ft == ST - 1), skip_group_check=True)
                        if tt == TPC - 1:
                            last.then_inc(act_used, 1)
                        if tt % 2 == 1:
                            next_part()

                for ft in range(1, ST):
                    if last_one and ft >= 2:
                        pe.wait_ge(banks_read, ft - 1)
                    else:
                        pe.wait_ge(gu_free, c * ST + (ft + 1))
                    gate_up(c, ft, next_part)
                pe.wait_ge(down_read, c * TPC + TPC)
                for ft in range(ST - 1):
                    down(ft)
                if last_one:
                    turn(0, 0)
                else:
                    pe.wait_ge(gu_free, c * ST + (ST + 1))
                    gate_up(c + 1, 0, next_part)
                down(ST - 1)

            PARTS = 24
            def round_total(c, n):
                if n % (PARTS // RPC) == 2:
                    total(c * RPC + n // (PARTS // RPC))

            with pe.Fori(0, NCH - 2) as c:
                chunk(c, lambda n: round_total(c, n))
            pe.wait_ge(scores_ready, 1)
            for j in range(2):
                nc.tensor.transpose(PS[6][:, j * P:(j + 1) * P], SCO[:, j * P:(j + 1) * P], ident[:]).then_inc(scores_turned, 1)

            def offsets_and_slots(n):
                if n < (ROUNDS - RPC * (NCH - 2)) * (PARTS // RPC):
                    round_total(NCH - 2, n)
                if n == 18:
                    pe.wait_ge(tails, 1)
                    M(CNT[:, 0:1], before[:], cntb[:, 0:1], start=True, stop=True)
                    M(CNT[:, 1:2], before[:], cntb[:, 1:2], start=True, stop=False)
                    M(CNT[:, 1:2], same[:], cntb[:, 0:1], start=False, stop=True).then_inc(tail_tot, 1)
                if n == 21:
                    pe.wait_ge(slots_ready, 1)
                    pe.wait_ge(scores_laid, 2)
                    for j in range(2):
                        nc.tensor.transpose(PS[6][:, j * P:(j + 1) * P], TMPA[:, j * P:(j + 1) * P], ident[:]).then_inc(slots_turned, 1)

            def token_numbers(n):
                if n in (9, 10):
                    half = n - 9
                    pe.wait_ge(onehots, half + 1)
                    ob = OB.rearrange("p (s t e) -> p s t e", s=16, e=NE)
                    for t in range(half * NT // 2, (half + 1) * NT // 2):
                        for g in range(2):
                            last = M(PS[7][:, g * P:(g + 1) * P], OA[:, (2 * t + g) * P:(2 * t + g + 1) * P], ob[:, :, t, g * 8:g * 8 + 8],
                                     start=(t == 0 and g == 0), stop=(t == NT - 1), skip_group_check=True)
                    if half == 1:
                        last.then_inc(ids_done, 1)
                if n == 11:
                    pe.wait_ge(ids_masked, 1)
                    M(PS[6][:, 0:2 * P], spread[:], IDH, start=True, stop=True).then_inc(ids_spread, 1)

            chunk(NCH - 2, offsets_and_slots)
            chunk(NCH - 1, token_numbers, last_one=True)
            pe.wait_ge(gu_free, SN + 2)

            def down(j, k):
                piece, sl = GUP + k // 2, slice(k % 2 * C, (k % 2 + 1) * C)
                a = slice(k * CAP + j * P, k * CAP + (j + 1) * P)
                return three(OUT[j][:, 0:C], (AH[:, a], AL[:, a]), (WH[:, piece, sl], WL[:, piece, sl]),
                             start=(k == 0), stop=(k == FT - 1))

            def expert(e, s, first=False, last_one=False):
                pe.wait_ge(xtlo_done, e + 1)
                for f in range(FT):
                    pe.wait_ge(w_lo, GUP * e + (f + 1))
                    pe.wait_ge(gu_free, SN + FT * e + (f - 1))
                    for g in range(2):
                        for k in range(H):
                            sl = slice(g * 2 * P + k * P, g * 2 * P + (k + 1) * P)
                            last = three(PS[f % 4][:, g * CAP:(g + 1) * CAP], (WH[:, f, sl], WL[:, f, sl]),
                                         (XTH[:, k, :], XTL[:, k, :]), start=(k == 0), stop=(k == H - 1))
                    last.then_inc(gu_done, 1)
                if first:
                    pe.wait_ge(down_read, TPC + NCH * TPC)
                else:
                    pe.wait_ge(y_biased, 2 * e)
                for k in range(FT):
                    if k == 2 and not last_one:
                        turn(e + 1, 1 - s)
                    pe.wait_ge(actlo_done, SN + FT * e + (k + 3))
                    if k % 2 == 0:
                        pe.wait_ge(wd_lo, DNP * e + (k // 2 + 1))
                    for j in range(1 if last_one else 2):
                        last = down(j, k)
                    if last_one and k == FT - 1:
                        last.then_inc(last_down, 1)
                    elif not last_one:
                        last.then_inc(act_used, 1)
                if last_one:
                    for k in range(FT):
                        last = down(1, k)
                    last.then_inc(last_down, 1)

            expert(0, 0, first=True)
            with pe.Fori(0, (NE - 2) // 2) as pair:
                for s in range(2):
                    expert(pair * 2 + (s + 1), 1 - s)
            expert(NE - 1, 1, last_one=True)


def kernel(**inputs):
    import numpy as np
    import concourse.bacc as bacc
    from concourse import mybir
    from concourse.bass_utils import run_bass_kernel_spmd as run

    A = {k: np.asarray(v) for k, v in inputs.items()}
    P, E = 128, 16

    def gate_up(g, u):
        w = np.stack([g, u], axis=-3)
        lead = w.shape[:-3]
        w = w.reshape(*lead, 2, -1, P, 2, P)
        n = len(lead)
        w = w.transpose(*range(n), n + 4, n + 1, n, n + 3, n + 2)
        return np.ascontiguousarray(w.reshape(*lead, P, -1))

    def down(w):
        lead = w.shape[:-2]
        n = len(lead)
        w = w.reshape(*lead, 256, -1, P).transpose(*range(n), n + 2, n + 1, n)
        return np.ascontiguousarray(w.reshape(*lead, P, -1))

    halves = lambda v: v.reshape(2, P).T
    arrays = {
        "x": A["x"],
        "ctx": np.ascontiguousarray(A["ctx_1024"].transpose(2, 0, 1).reshape(2, P, 8, 256).transpose(1, 2, 0, 3)),
        "wu": np.ascontiguousarray(np.concatenate([halves(A["L0_xattn_w"].reshape(-1)), halves(A["L0_xattn_u"].reshape(-1))], axis=1)),
        "g": np.ascontiguousarray(np.broadcast_to(np.concatenate([A["g_xattn"], A["g_ffn"]]), (P, 2))),
        "gatew": np.ascontiguousarray(A["L0_ffn_gate_w"].reshape(E, 2, P).transpose(2, 1, 0)),
        "shgu": gate_up(A["L0_ffn_sh_gate_w"], A["L0_ffn_sh_up_w"]),
        "shd": down(A["L0_ffn_sh_down_w"]),
        "gu": gate_up(A["L0_ffn_gw"], A["L0_ffn_up_w"]),
        "dn": down(A["L0_ffn_down_w"]),
        "fb": np.ascontiguousarray(np.concatenate([A["L0_ffn_gb"].reshape(E, 8, P).transpose(0, 2, 1),
                                                   A["L0_ffn_up_b"].reshape(E, 8, P).transpose(0, 2, 1)], axis=2)),
        "db": A["L0_ffn_down_b"],
    }
    nc = bacc.Bacc("TRN2", target_bir_lowering=False, num_devices=1)
    aps = [nc.dram_tensor(f"in_{k}", a.shape, mybir.dt.from_np(a.dtype), kind="ExternalInput").ap() for k, a in arrays.items()]
    out = nc.dram_tensor("out_0", (8, 256, 256), mybir.dt.float32, kind="ExternalOutput").ap()
    flamingo_layer(nc, *aps, out)
    r = run(nc, [{f"in_{k}": a for k, a in arrays.items()}], core_ids=[0])
    return r.results[0]["out_0"]
```
